# Optimizing a Trainium2 kernel written in Bass

```python
import numpy as np
import jax
import jax.numpy as jnp

def _softmax(x, axis=-1):
    return jax.nn.softmax(x, axis=axis)

def _gelu(x):
    return jax.nn.gelu(x, approximate=True)

def _silu(x):
    return jax.nn.silu(x)

def _sigmoid(x):
    return jax.nn.sigmoid(x)

def _layernorm(x, axis=-1, eps=1e-05):
    m = jnp.mean(x, axis=axis, keepdims=True)
    v = jnp.var(x, axis=axis, keepdims=True)
    return (x - m) / jnp.sqrt(v + eps)

def _scatter_add(tgt, idx, src, axis=0):
    return tgt.at[idx].add(src)

def _segment_sum(src, seg, n):
    return jax.ops.segment_sum(src, seg, n)
kernel_name = 'mk_vit_tower_cls_d1_tok_img256_r4_9c9e9e'

def setup_inputs(seed: int=0):
    np.random.seed(seed)
    _w = jnp.asarray

    def _rec_inputs():
        import jax
        import jax.numpy as jnp
        _rk = jax.random.key(seed)
        x = -0.000209053 + 0.999977 * jax.random.normal(jax.random.fold_in(_rk, 1), (4, 64, 56, 56), jnp.float32)
        cls_tok = 0.02 * jax.random.normal(jax.random.fold_in(_rk, 5), (1, 1, 64), jnp.float32)
        return (x, cls_tok)
    x, cls_tok = _rec_inputs()

    def _L0_tok_setup():
        import jax, jax.numpy as jnp
        import numpy as np
        B, EMB, HT, WD = (32, 64, 56, 56)
        NH, WS, SHIFTED = (8, 4, True)

        def _rel_indices(ws):
            coords = np.array([[i, j] for i in range(ws) for j in range(ws)])
            rel = coords[None, :, :] - coords[:, None, :] + ws - 1
            return jnp.asarray(rel)

        def _shift_masks(ws):
            m = np.zeros((ws * ws, ws * ws), np.float32)
            s = ws * (ws // 2)
            m[-s:, :-s] = -np.inf
            m[:-s, -s:] = -np.inf
            col = m.reshape(ws, ws, ws, ws).transpose(1, 0, 3, 2).reshape(ws * ws, ws * ws)
            return (jnp.asarray(m), jnp.asarray(col))
        key = jax.random.key(seed)
        ks = jax.random.split(key, 6)
        x = jax.random.normal(ks[0], (B, EMB, HT, WD), jnp.float32)
        s = 1.0 / np.sqrt(EMB)
        w1 = jax.random.uniform(ks[1], (3 * EMB, EMB), jnp.float32, -s, s)
        b1 = jax.random.uniform(ks[2], (3 * EMB,), jnp.float32, -s, s)
        w2 = jax.random.uniform(ks[3], (EMB, EMB), jnp.float32, -s, s)
        b2 = jax.random.uniform(ks[4], (EMB,), jnp.float32, -s, s)
        pos_emb = jax.random.normal(ks[5], (2 * WS - 1, 2 * WS - 1), jnp.float32)
        return {'x': x, 'w1': w1, 'b1': b1, 'w2': w2, 'b2': b2, 'pos_emb': pos_emb}
    _L0_tok_all = _L0_tok_setup()
    _L0_tok_in = {k: v for k, v in _L0_tok_all.items() if k in ('w1', 'b1', 'w2', 'b2', 'pos_emb')}
    del _L0_tok_all

    def _L0_attn_setup():
        import jax, jax.numpy as jnp
        import numpy as np
        GAMMA = 0.96875
        ROPE_THETA = 10000.0

        def _rope(x):
            B, S, d = x.shape
            inv_freq = 1.0 / ROPE_THETA ** (jnp.arange(0, d, 2, dtype=jnp.float32) / d)
            angles = jnp.arange(S, dtype=jnp.float32)[:, None] * inv_freq[None, :]
            cos = jnp.cos(angles).astype(x.dtype)
            sin = jnp.sin(angles).astype(x.dtype)
            xs = x.reshape(B, S, d // 2, 2)
            x0, x1 = (xs[..., 0], xs[..., 1])
            out = jnp.stack([x0 * cos - x1 * sin, x1 * cos + x0 * sin], axis=-1)
            return out.reshape(B, S, d)

        def _decay_mask(S, dtype):
            n = jnp.arange(S)[:, None]
            m = jnp.arange(S)[None, :]
            diff = n - m
            D = jnp.exp(jnp.maximum(diff, 0).astype(jnp.float32) * np.log(GAMMA))
            return jnp.where(diff >= 0, D, 0.0).astype(dtype)
        key = jax.random.key(seed)
        k1, k2, k3, k4 = jax.random.split(key, 4)
        H = 64
        X = jax.random.normal(k1, (4, 2048, H), dtype=jnp.float32)
        W_Q = jax.random.normal(k2, (H, H), dtype=jnp.float32) / H
        W_K = jax.random.normal(k3, (H, H), dtype=jnp.float32) / H
        W_V = jax.random.normal(k4, (H, H), dtype=jnp.float32) / H
        return {'X': X, 'W_Q': W_Q, 'W_K': W_K, 'W_V': W_V}
    _L0_attn_all = _L0_attn_setup()
    _L0_attn_in = {k: v for k, v in _L0_attn_all.items() if k in ('W_Q', 'W_K', 'W_V')}
    del _L0_attn_all

    def _L0_ffn_setup():
        import jax, jax.numpy as jnp
        import numpy as np
        B, S, H, F, E, K = (8, 1024, 64, 128, 16, 2)
        EPS = 1e-05
        key = jax.random.key(seed)
        ks = jax.random.split(key, 9)
        sc = 0.02
        return {'x': jax.random.normal(ks[0], (B, S, H), dtype=jnp.float32), 'gate_w': jax.random.normal(ks[1], (H, E), dtype=jnp.float32) * sc, 'gate_b': jnp.zeros((E,), dtype=jnp.float32), 'w1': jax.random.normal(ks[2], (E, H, F), dtype=jnp.float32) * sc, 'b1': jnp.zeros((E, F), dtype=jnp.float32), 'w2': jax.random.normal(ks[3], (E, F, H), dtype=jnp.float32) * sc, 'b2': jnp.zeros((E, H), dtype=jnp.float32), 'gamma': jnp.ones((H,), dtype=jnp.float32), 'beta': jnp.zeros((H,), dtype=jnp.float32)}
    _L0_ffn_all = _L0_ffn_setup()
    _L0_ffn_in = {k: v for k, v in _L0_ffn_all.items() if k in ('gate_w', 'gate_b', 'w1', 'b1', 'w2', 'b2', 'gamma', 'beta')}
    del _L0_ffn_all
    return {'x': x, 'cls_tok': cls_tok, 'L0_tok_w1': _L0_tok_in['w1'], 'L0_tok_b1': _L0_tok_in['b1'], 'L0_tok_w2': _L0_tok_in['w2'], 'L0_tok_b2': _L0_tok_in['b2'], 'L0_tok_pos_emb': _L0_tok_in['pos_emb'], 'L0_attn_W_Q': _L0_attn_in['W_Q'], 'L0_attn_W_K': _L0_attn_in['W_K'], 'L0_attn_W_V': _L0_attn_in['W_V'], 'L0_ffn_gate_w': _L0_ffn_in['gate_w'], 'L0_ffn_gate_b': _L0_ffn_in['gate_b'], 'L0_ffn_w1': _L0_ffn_in['w1'], 'L0_ffn_b1': _L0_ffn_in['b1'], 'L0_ffn_w2': _L0_ffn_in['w2'], 'L0_ffn_b2': _L0_ffn_in['b2'], 'L0_ffn_gamma': _L0_ffn_in['gamma'], 'L0_ffn_beta': _L0_ffn_in['beta']}

def reference(x, cls_tok, L0_tok_w1, L0_tok_b1, L0_tok_w2, L0_tok_b2, L0_tok_pos_emb, L0_attn_W_Q, L0_attn_W_K, L0_attn_W_V, L0_ffn_gate_w, L0_ffn_gate_b, L0_ffn_w1, L0_ffn_b1, L0_ffn_w2, L0_ffn_b2, L0_ffn_gamma, L0_ffn_beta):
    import jax
    import jax.numpy as jnp

    def _L0_tok_ref(x, w1, b1, w2, b2, pos_emb):
        import jax, jax.numpy as jnp
        import numpy as np
        B, EMB, HT, WD = (32, 64, 56, 56)
        NH, WS, SHIFTED = (8, 4, True)

        def _rel_indices(ws):
            coords = np.array([[i, j] for i in range(ws) for j in range(ws)])
            rel = coords[None, :, :] - coords[:, None, :] + ws - 1
            return jnp.asarray(rel)

        def _shift_masks(ws):
            m = np.zeros((ws * ws, ws * ws), np.float32)
            s = ws * (ws // 2)
            m[-s:, :-s] = -np.inf
            m[:-s, -s:] = -np.inf
            col = m.reshape(ws, ws, ws, ws).transpose(1, 0, 3, 2).reshape(ws * ws, ws * ws)
            return (jnp.asarray(m), jnp.asarray(col))
        b, c, ht, wd = x.shape
        ws, nh = (WS, NH)
        e = c // nh
        xt = x.reshape(b, c, ht * wd).transpose(0, 2, 1)
        qkv = xt @ w1.T + b1
        qkv = qkv.reshape(b, ht, wd, c, 3)
        if SHIFTED:
            qkv = jnp.roll(qkv, (-ws // 2, -ws // 2), axis=(1, 2))
        Wh, Ww = (ht // ws, wd // ws)
        qkv = qkv.reshape(b, Wh, ws, Ww, ws, e, nh, 3)
        qkv = qkv.transpose(0, 6, 1, 3, 2, 4, 5, 7).reshape(b, nh, Wh, Ww, ws * ws, e, 3)
        Q, K, V = (qkv[..., 0], qkv[..., 1], qkv[..., 2])
        scale = jnp.sqrt(jnp.float32(c / nh))
        wei = jnp.einsum('bhijpe,bhijqe->bhijpq', Q, K) / scale
        rel = _rel_indices(ws)
        wei = wei + pos_emb[rel[..., 0], rel[..., 1]]
        if SHIFTED:
            row_mask, col_mask = _shift_masks(ws)
            wei = wei.at[:, :, -1, :].add(row_mask)
            wei = wei.at[:, :, :, -1].add(col_mask)
        attn = jax.nn.softmax(wei, axis=-1)
        out = jnp.einsum('bhijpq,bhijqe->bhijpe', attn, V)
        out = out.reshape(b, nh, Wh, Ww, ws, ws, e)
        out = out.transpose(0, 2, 4, 3, 5, 1, 6).reshape(b, ht, wd, nh * e)
        out = out.reshape(b, ht * wd, c)
        return out @ w2.T + b2

    def _L0_attn_ref(X, W_Q, W_K, W_V):
        import jax, jax.numpy as jnp
        import numpy as np
        GAMMA = 0.96875
        ROPE_THETA = 10000.0

        def _rope(x):
            B, S, d = x.shape
            inv_freq = 1.0 / ROPE_THETA ** (jnp.arange(0, d, 2, dtype=jnp.float32) / d)
            angles = jnp.arange(S, dtype=jnp.float32)[:, None] * inv_freq[None, :]
            cos = jnp.cos(angles).astype(x.dtype)
            sin = jnp.sin(angles).astype(x.dtype)
            xs = x.reshape(B, S, d // 2, 2)
            x0, x1 = (xs[..., 0], xs[..., 1])
            out = jnp.stack([x0 * cos - x1 * sin, x1 * cos + x0 * sin], axis=-1)
            return out.reshape(B, S, d)

        def _decay_mask(S, dtype):
            n = jnp.arange(S)[:, None]
            m = jnp.arange(S)[None, :]
            diff = n - m
            D = jnp.exp(jnp.maximum(diff, 0).astype(jnp.float32) * np.log(GAMMA))
            return jnp.where(diff >= 0, D, 0.0).astype(dtype)
        B, S, _ = X.shape
        D = _decay_mask(S, X.dtype)
        Q = _rope(X @ W_Q)
        K = _rope(X @ W_K)
        V = X @ W_V
        ret = jnp.einsum('bqd,bkd->bqk', Q, K) * D[None]
        return ret @ V

    def _L0_ffn_ref(x, gate_w, gate_b, w1, b1, w2, b2, gamma, beta):
        import jax, jax.numpy as jnp
        import numpy as np
        B, S, H, F, E, K = (8, 1024, 64, 128, 16, 2)
        EPS = 1e-05
        gate_logits = x @ gate_w + gate_b
        topk_vals, topk_idx = jax.lax.top_k(gate_logits, K)
        topk_w = jax.nn.softmax(topk_vals, axis=-1)
        h = jax.nn.relu(jnp.einsum('bsh,ehf->bsef', x, w1) + b1)
        expert_out = jnp.einsum('bsef,efh->bseh', h, w2) + b2
        sel = jnp.take_along_axis(expert_out, topk_idx[:, :, :, None], axis=2)
        moe = jnp.sum(topk_w[..., None] * sel, axis=2)
        y = x + moe
        mu = jnp.mean(y, axis=-1, keepdims=True)
        var = jnp.var(y, axis=-1, keepdims=True)
        return (y - mu) / jnp.sqrt(var + EPS) * gamma + beta
    h = _L0_tok_ref(x, L0_tok_w1, L0_tok_b1, L0_tok_w2, L0_tok_b2, L0_tok_pos_emb)
    h = jnp.concatenate([jnp.broadcast_to(cls_tok, (h.shape[0], 1, h.shape[2])), h], axis=1)
    h = h + _L0_attn_ref(_layernorm(h, axis=-1), L0_attn_W_Q, L0_attn_W_K, L0_attn_W_V)
    h = h + _L0_ffn_ref(_layernorm(h, axis=-1), L0_ffn_gate_w, L0_ffn_gate_b, L0_ffn_w1, L0_ffn_b1, L0_ffn_w2, L0_ffn_b2, L0_ffn_gamma, L0_ffn_beta)
    return h

_drawn_inputs = setup_inputs


def setup_inputs(seed=0):
    import zlib

    import numpy as np

    out = dict(_drawn_inputs(seed))
    spreads = {'L0_ffn_gate_b': (0.0, 0.1),
     'L0_ffn_b1': (0.0, 0.8),
     'L0_ffn_b2': (0.0, 0.1),
     'L0_ffn_gamma': (1.0, 0.2),
     'L0_ffn_beta': (0.0, 0.1)}
    factors = {'cls_tok': 29.424, 'L0_ffn_w1': 4.706, 'L0_ffn_w2': 3.63}
    for name, (base, spread) in spreads.items():
        noise = np.random.default_rng([zlib.crc32(name.encode()), seed]).standard_normal(out[name].shape)
        drawn = base * np.exp(spread * noise) if base else spread * noise
        out[name] = jnp.asarray(drawn.astype(out[name].dtype))
    for name, factor in factors.items():
        out[name] = (out[name] * factor).astype(out[name].dtype)
    return out
```

```python
from contextlib import ExitStack

import numpy as np

import concourse.bass as bass
from concourse import mybir

F32 = mybir.dt.float32
F32R = mybir.dt.float32r
U32 = mybir.dt.uint32
ALU = mybir.AluOpType
ACT = mybir.ActivationFunctionType
AX = mybir.AxisListType

IMAGES, EMB, SIDE = 4, 64, 56
HEADS, WIN, HD = 8, 4, 8
EXPERTS, FF, TOP = 16, 128, 2
GAMMA, THETA, EPS = 0.96875, 10000.0, 1e-5
QUERIES = WIN * WIN
ROWS = 2 * WIN
BT = ROWS * SIDE
BLOCKS = SIDE // ROWS
ALL_BLOCKS = IMAGES * BLOCKS
CT = 2 * SIDE
CHUNKS = BT // CT
PAIRS = BT // QUERIES // 2
WPT = CT // QUERIES
HALF = BT // 2
SEQ = 1 + SIDE * SIDE
MASKED = -1e30


def broadcast(ap, axis, n):
    ap = ap.unsqueeze(axis)
    shape = list(ap.shape)
    shape[axis] = n
    return ap.broadcast_to(shape)


def build_tower(nc, I, y):
    ctx = ExitStack()
    with ctx:
        def sb(name, shape, dt=F32):
            return ctx.enter_context(nc.sbuf_tensor(name, shape, dt))

        def ps(name, shape):
            return ctx.enter_context(nc.psum_tensor(name, shape, F32))

        def sem(name):
            return ctx.enter_context(nc.semaphore(name))

        qk_raw = sb("qk_raw", [128, 2, EMB])
        q_even_odd = [[sb(f"q_w{p}{s}", [128, 128], F32R) for s in "hl"] for p in "eo"]
        k_even_odd = [[sb(f"k_w{p}{s}", [128, 128], F32R) for s in "hl"] for p in "eo"]
        v_raw = sb("v_raw", [128, EMB])
        v_w = [sb(f"v_w{s}", [128, EMB], F32R) for s in "hl"]
        qk_bias = sb("qk_bias", [128, 2])
        q_bias = sb("q_bias", [128, 1])
        v_bias = sb("v_bias", [CT, EMB])
        out_w = sb("out_w", [EMB + 1, EMB])
        win_bias = sb("win_bias", [128, BLOCKS, 4, QUERIES])
        pos_bias = sb("pos_bias", [128, QUERIES])
        head_of_channel = sb("head_of_channel", [128, HEADS])
        head_columns = sb("head_columns", [128, EMB])
        pick = sb("pick", [CT, WPT, 128])
        ident = sb("ident", [128, 128])
        r_raw = sb("r_raw", [128, 5, EMB])
        r_w = [sb(f"r_w{s}", [128, 5, EMB], F32R) for s in "hl"]
        cos_t = sb("cos_t", [128, 1 + SIDE * SIDE])
        sin_t = sb("sin_t", [128, 1 + SIDE * SIDE])
        cls_cos = sb("cls_cos", [128, BT])
        cls_sin = sb("cls_sin", [128, BT])
        decay = sb("decay", [CT, 2, CT])
        key_decay = sb("key_decay", [CT, 2])
        query_decay = sb("query_decay", [CT, 1])
        gate_raw = sb("gate_raw", [128, EXPERTS])
        gate_w = [sb(f"gate_w{s}", [128, EXPERTS], F32R) for s in "hl"]
        gate_bias = sb("gate_bias", [CT, EXPERTS])
        expert_ids = sb("expert_ids", [CT, EXPERTS])
        up_raw = sb("up_raw", [128, EXPERTS, FF])
        up_w = [sb(f"up_w{s}", [128, EXPERTS, FF], F32R) for s in "hl"]
        up_bias = sb("up_bias", [FF, EXPERTS])
        down_w = sb("down_w", [FF, EXPERTS, EMB])
        b2_raw = sb("b2_raw", [128, 128])
        b2_w = [sb(f"b2_w{s}", [128, 128], F32R) for s in "hl"]
        sel_row = sb("sel_row", [128, EXPERTS])
        sel = sb("sel", [128, EXPERTS, 128], F32R)
        fold = sb("fold", [128, EMB])
        ln_gamma = sb("ln_gamma", [CT, EMB])
        ln_beta = sb("ln_beta", [CT, EMB])
        power = sb("power", [CT, CHUNKS])
        eps_t = sb("eps_t", [CT, CHUNKS])

        x_in = sb("x_in", [128, BT])
        x_split = sb("x_split", [128, BT], F32R)
        k_sb = sb("k_sb", [128, HALF])
        q_zero = sb("q_zero", [128, PAIRS, 2, QUERIES])
        k_heads = sb("k_heads", [128, PAIRS, HEADS, QUERIES])
        v_tok = sb("v_tok", [CT, 4, EMB])
        v_heads = sb("v_heads", [128, WPT, 4, EMB])
        logits = sb("logits", [128, 4, HEADS, QUERIES])
        shifted = sb("shifted", [128, 4, HEADS, QUERIES])
        probs = sb("probs", [128, 4, HEADS, QUERIES])
        probs_n = sb("probs_n", [128, 4, HEADS, QUERIES])
        row_max = sb("row_max", [128, 4, HEADS])
        row_sum = sb("row_sum", [128, 4, HEADS])
        row_inv = sb("row_inv", [128, 4, HEADS])
        probs_t = sb("probs_t", [128, BT + 64])
        att_t = sb("att_t", [EMB + 1, BT])
        h1 = sb("h1", [CT, CHUNKS, EMB])
        xn = sb("xn", [CT, CHUNKS, 2, EMB])
        stats = sb("stats", [CT, CHUNKS, 6])
        mean_var = sb("mean_var", [CT, CHUNKS, 5])
        var_eps = sb("var_eps", [CT, CHUNKS])
        rstd = sb("rstd", [CT, CHUNKS])
        centred = sb("centred", [CT, CHUNKS, EMB])
        xn_split = sb("xn_split", [128, BT], F32R)
        rot_cos = sb("rot_cos", [128, BT])
        rot_sin = sb("rot_sin", [128, BT])
        q_t = sb("q_t", [EMB, BT])
        k_t = sb("k_t", [EMB, BT])
        v2 = sb("v2", [CT, CHUNKS, EMB])
        att = sb("att", [CT, CHUNKS, CT])
        k_dec = sb("k_dec", [CT, CHUNKS, EMB])
        state = sb("state", [EMB, CHUNKS + 1, EMB])
        state_cls = sb("state_cls", [EMB, EMB])
        h1_intra = sb("h1_intra", [CT, CHUNKS, EMB])
        h2 = sb("h2", [CT, CHUNKS, EMB])
        x2 = sb("x2", [CT, CHUNKS, 2, EMB])
        gate_logits = sb("gate_logits", [CT, CHUNKS, EXPERTS])
        top_val = sb("top_val", [CT, CHUNKS, 8])
        top_idx = sb("top_idx", [CT, CHUNKS, 8], U32)
        top_id = sb("top_id", [CT, CHUNKS, 2])
        top_diff = sb("top_diff", [CT, CHUNKS])
        top_exp = sb("top_exp", [CT, CHUNKS])
        top_den = sb("top_den", [CT, CHUNKS])
        top_w = sb("top_w", [CT, 2, CHUNKS])
        one_hot = sb("one_hot", [CT, 2, CHUNKS, EXPERTS])
        gates_a = sb("gates_a", [CT, 2, CHUNKS, EXPERTS])
        gates = sb("gates", [CT, CHUNKS, EXPERTS])
        x2_split = sb("x2_split", [128, BT], F32R)
        gates_split = sb("gates_split", [128, BT], F32R)
        h2_keep = sb("h2_keep", [CT, CHUNKS, EMB])
        x2_keep = sb("x2_keep", [CT, CHUNKS, EMB])
        hidden = sb("hidden", [128, 2, BT])
        gated = sb("gated", [128, 2, BT])
        moe_sb = sb("moe_sb", [128, BT])
        res = sb("res", [CT, CHUNKS, EMB])
        stats3 = sb("stats3", [CT, CHUNKS, 6])
        mean_var3 = sb("mean_var3", [CT, CHUNKS, 5])
        var_eps3 = sb("var_eps3", [CT, CHUNKS])
        rstd3 = sb("rstd3", [CT, CHUNKS])
        centred3 = sb("centred3", [CT, CHUNKS, EMB])
        normed3 = sb("normed3", [CT, CHUNKS, EMB])
        h3 = sb("h3", [CT, CHUNKS, EMB])

        W0, W1, W2 = (ps(f"work{i}", [128, 512]) for i in range(3))
        up_ps = [ps(f"up{i}", [128, 512]) for i in range(2)]
        gate_ps = [ps(f"gate{i}", [128, 512]) for i in range(2)]
        moe_ps = ps("moe", [128, 512])

        loaded = sem("loaded")
        filled = sem("filled")
        setup = sem("setup")
        x_loaded = sem("x_loaded")
        x_high = sem("x_high")
        x_ready = sem("x_ready")
        qk_done = sem("qk_done")
        v_done = sem("v_done")
        q_ready = sem("q_ready")
        k_copied = sem("k_copied")
        k_ready = sem("k_ready")
        v_ready = sem("v_ready")
        s_done = sem("s_done")
        chain1 = sem("chain1")
        shifted_ready = sem("shifted_ready")
        exp_ready = sem("exp_ready")
        probs_ready = sem("probs_ready")
        probs_turned = sem("probs_turned")
        probs_t_ready = sem("probs_t_ready")
        v_spread = sem("v_spread")
        v_masked = sem("v_masked")
        av_done = sem("av_done")
        att_t_ready = sem("att_t_ready")
        h1_done = sem("h1_done")
        h1_ready = sem("h1_ready")
        chain2 = sem("chain2")
        var_ready = sem("var_ready")
        rstd_ready = sem("rstd_ready")
        pool_chain2 = sem("pool_chain2")
        pool_chain3 = sem("pool_chain3")
        xn_ready = sem("xn_ready")
        xn_turned = sem("xn_turned")
        xn_high = sem("xn_high")
        xn_split_ready = sem("xn_split_ready")
        rqk_done = sem("rqk_done")
        rv_done = sem("rv_done")
        v2_ready = sem("v2_ready")
        rot_ready = sem("rot_ready")
        kq_done = sem("kq_done")
        kt_turned = sem("kt_turned")
        att_ready = sem("att_ready")
        k_dec_ready = sem("k_dec_ready")
        state_done = sem("state_done")
        state_ready = sem("state_ready")
        ret_done = sem("ret_done")
        h2_ready = sem("h2_ready")
        x2_ready = sem("x2_ready")
        x2_turned = sem("x2_turned")
        x2_high = sem("x2_high")
        x2_split_ready = sem("x2_split_ready")
        gl_done = sem("gl_done")
        gl_ready = sem("gl_ready")
        diff_ready = sem("diff_ready")
        gexp_ready = sem("gexp_ready")
        gates_ready = sem("gates_ready")
        gates_turned = sem("gates_turned")
        gates_high = sem("gates_high")
        gates_split_ready = sem("gates_split_ready")
        kept = sem("kept")
        up_done = sem("up_done")
        gate_done = sem("gate_done")
        hidden_ready = sem("hidden_ready")
        gated_ready = sem("gated_ready")
        down_done = sem("down_done")
        moe_copied = sem("moe_copied")
        moe_folded = sem("moe_folded")
        chain3 = sem("chain3")
        chain_s = sem("chain_s")
        var3_ready = sem("var3_ready")
        rstd3_ready = sem("rstd3_ready")
        normed3_ready = sem("normed3_ready")
        h3_ready = sem("h3_ready")
        stored = sem("stored")

        CH1, CH2, CH3, CHS, CHP2, CHP3 = 4, 18, 5, 4, 2, 2

        def link(eng, s, n, per):
            count = [0]

            def wait_for(ins):
                count[0] += 1
                assert count[0] <= per
                ins.then_inc(s, 1)
                eng.wait_ge(s, n * per + count[0])
            return wait_for

        loads = []
        for dst, name in (
            (qk_raw[0:64], "w_qk"), (qk_raw[64:128], "w_qk"), (v_raw[0:64], "w_v"), (v_raw[64:128], "w_v"),
            (qk_bias[0:64], "b_qk"), (qk_bias[64:128], "b_qk"), (v_bias[:], "b_v"), (out_w[:], "w_out"),
            (win_bias[:].rearrange("p a b c -> p (a b c)"), "win_mask"), (pos_bias[:], "pos"),
            (head_of_channel[:], "head_of_channel"), (head_columns[:], "head_columns"),
            (pick[:].rearrange("p a b -> p (a b)"), "pick"), (ident[:], "ident"),
            (r_raw[0:64], "w_ret"), (r_raw[64:128], "w_ret"), (cos_t[:], "cos"), (sin_t[:], "sin"),
            (decay[:].rearrange("p a b -> p (a b)"), "decay"), (key_decay[:], "key_decay"),
            (query_decay[:], "query_decay"), (gate_raw[0:64], "w_gate"), (gate_raw[64:128], "w_gate"),
            (gate_bias[:], "b_gate"), (expert_ids[:], "expert_ids"),
            (up_raw[0:64], "w_up"), (up_raw[64:128], "w_up"), (up_bias[:], "b_up"), (down_w[:], "w_down"),
            (sel_row[:], "sel_row"), (fold[:], "fold"), (ln_gamma[:], "gamma"), (ln_beta[:], "beta"),
            (h1[:].rearrange("p c n -> p (c n)"), "cls"),
        ):
            loads.append((dst, I[name]))
        B2_LOADS = 2
        N_LOADED = 16 * (len(loads) + B2_LOADS)
        N_FILLED = 5
        N_SETUP = 22

        block = ctx.enter_context(nc.Block())

        @block.sync
        def _(sp):
            for dst, src in loads:
                sp.dma_start(dst, src).then_inc(loaded, 16)
            sp.wait_ge(filled, N_FILLED)
            for row in (0, 32):
                sp.dma_start(b2_raw[row:row + EXPERTS, 0:EMB], I["b_down"]).then_inc(loaded, 16)

            def load_x(it):
                for half in (0, 64):
                    sp.dma_start(x_in[half:half + 64, :],
                                 I["x"][bass.ds(it, 1)].rearrange("o c t -> (o c) t")).then_inc(x_loaded, 16)

            def store(n):
                sp.wait_ge(h3_ready, n + 1)
                sp.dma_start(y[bass.ds(n * CHUNKS, CHUNKS)].rearrange("c t n -> t c n"), h3[:]).then_inc(stored, 16)

            load_x(0)
            with sp.Fori(0, ALL_BLOCKS - 1) as it:
                sp.wait_ge(x_ready, it + 1)
                load_x(it + 1)
                store(it)
            store(ALL_BLOCKS - 1)
            store(ALL_BLOCKS)
            sp.wait_ge(stored, 16 * (ALL_BLOCKS + 2))

        @block.tensor
        def _(pe):
            mm = pe.matmul

            def w_project_qk(it, n):
                pe.wait_ge(x_ready, it + 1)
                pe.wait_ge(gl_ready, n)
                for out, w in ((W0[:, 0:HALF], q_even_odd), (W0[:, HALF:BT], k_even_odd)):
                    for k in range(4):
                        last = mm(out, w[k // 2][k % 2][:], x_split[:, (k // 2) * HALF:(k // 2 + 1) * HALF],
                                  start=(k == 0), stop=(k == 3))
                last.then_inc(qk_done, 1)

            def w_project_v(it, n):
                pe.wait_ge(gates_split_ready, n)
                for t in range(4):
                    for s in range(2):
                        last = mm(W1[0:CT, t * EMB:(t + 1) * EMB], x_split[:, t * CT:(t + 1) * CT], v_w[s][:],
                                  start=(s == 0), stop=(s == 1))
                last.then_inc(v_done, 1)

            def w_scores(it, n):
                pe.wait_ge(q_ready, 2 * it + 2)
                pe.wait_ge(k_ready, it + 1)
                pe.wait_ge(x2_split_ready, n)
                for g in range(4):
                    for c in range(4):
                        p = 4 * g + c if 4 * g + c < PAIRS else 4 * g + c - 2
                        last = mm(W2[32 * c:32 * c + 32, g * 128:(g + 1) * 128],
                                  q_zero[:, p].rearrange("p w q -> p (w q)"),
                                  k_heads[:, p].rearrange("p h q -> p (h q)"), start=True, stop=True)
                last.then_inc(s_done, 1)

            def w_spread_v(it, j):
                pe.wait_ge(v_ready, it + 1)
                if j == 1:
                    pe.wait_ge(chain1, CH1 * it + 1)
                if j >= 2:
                    pe.wait_ge(v_masked, 4 * it + j - 1)
                W = (W1, W2)[j % 2]
                for k in range(2 * j, min(2 * j + 2, WPT)):
                    last = mm(W[:, (k % 2) * 256:(k % 2) * 256 + 256], pick[:, k, :],
                              v_tok[:].rearrange("p t n -> p (t n)"), start=True, stop=True)
                last.then_inc(v_spread, 1)

            def w_turn_probs(it):
                pe.wait_ge(probs_ready, it + 1)
                for g in range(4):
                    last = pe.transpose(W0[:, g * 128:(g + 1) * 128],
                                        probs_n[:, g].rearrange("p h q -> p (h q)"), ident[:])
                last.then_inc(probs_turned, 1)

            def w_values(it):
                pe.wait_ge(probs_t_ready, it + 1)
                pe.wait_ge(v_masked, 4 * it + 4)
                for p in range(PAIRS):
                    wr, k = p // WPT, p % WPT
                    for odd in range(2):
                        col = (p // 4) * 128 + (p % 4) * 32 + odd * QUERIES
                        out = W1[64 * odd:64 * odd + 64, wr * HALF:(wr + 1) * HALF].rearrange(
                            "p (a c b) -> p a c b", a=WIN, b=WIN)[:, :, 2 * k + odd, :]
                        last = mm(out, v_heads[:, k, 2 * odd + wr, :], probs_t[:, col:col + QUERIES],
                                  start=True, stop=True)
                last.then_inc(av_done, 1)

            def w_project_out(it):
                pe.wait_ge(att_t_ready, 2 * it + 2)
                for c in range(CHUNKS):
                    last = mm(W2[0:CT, c * EMB:(c + 1) * EMB], att_t[:, c * CT:(c + 1) * CT], out_w[:],
                              start=True, stop=True)
                last.then_inc(h1_done, 1)

            def r_turn(src, W, n, ready, count, done):
                pe.wait_ge(ready, count)
                for c in range(CHUNKS):
                    last = pe.transpose(W[:, c * CT:(c + 1) * CT], src[:, c].rearrange("p a n -> p (a n)"),
                                        ident[0:CT, 0:CT])
                last.then_inc(done, 1)

            def r_project(n):
                pe.wait_ge(xn_split_ready, n + 1)
                for k, W in ((0, W1), (1, W2)):
                    for s in range(2):
                        last = mm(W[:, 0:BT], r_w[s][:, 2 * k:2 * k + 2].rearrange("p a b -> p (a b)"),
                                  xn_split[:], start=(s == 0), stop=(s == 1))
                last.then_inc(rqk_done, 1)
                for c in range(CHUNKS):
                    for s in range(2):
                        last = mm(W0[0:CT, c * EMB:(c + 1) * EMB], xn_split[:, c * CT:(c + 1) * CT],
                                  r_w[s][:, 4], start=(s == 0), stop=(s == 1))
                last.then_inc(rv_done, 1)

            def r_scores(n):
                pe.wait_ge(rot_ready, n + 1)
                for c in range(CHUNKS):
                    cols = slice(c * CT, (c + 1) * CT)
                    last = mm(W1[0:CT, cols], k_t[:, cols], q_t[:, cols], start=True, stop=True)
                last.then_inc(kq_done, 1)
                for c in range(CHUNKS):
                    last = pe.transpose(W2[0:CT, c * EMB:(c + 1) * EMB], k_t[:, c * CT:(c + 1) * CT],
                                        ident[0:EMB, 0:EMB])
                last.then_inc(kt_turned, 1)

            def r_state(n, rows):
                pe.wait_ge(v2_ready, n + 1)
                pe.wait_ge(k_dec_ready, n + 1)
                for c in range(CHUNKS):
                    last = mm(W0[0:EMB, c * EMB:(c + 1) * EMB], k_dec[0:rows, c], v2[0:rows, c],
                              start=True, stop=True)
                last.then_inc(state_done, 1)

            def r_output(n):
                pe.wait_ge(att_ready, n + 1)
                for c in range(CHUNKS):
                    mm(W1[0:CT, c * EMB:(c + 1) * EMB], att[:, c], v2[:, c], start=True, stop=True)
                pe.wait_ge(state_ready, n + 1)
                for c in range(CHUNKS):
                    last = mm(W1[0:CT, 256 + c * EMB:256 + (c + 1) * EMB], q_t[:, c * CT:(c + 1) * CT],
                              state[:, c], start=True, stop=True)
                last.then_inc(ret_done, 1)

            def r_gate(n):
                pe.wait_ge(x2_split_ready, n + 1)
                for c in range(CHUNKS):
                    for s in range(2):
                        last = mm(W0[0:CT, c * EXPERTS:(c + 1) * EXPERTS], x2_split[:, c * CT:(c + 1) * CT],
                                  gate_w[s][:], start=(s == 0), stop=(s == 1))
                last.then_inc(gl_done, 1)

            def r_turn_gates(n):
                pe.wait_ge(gates_ready, n + 1)
                for c in range(CHUNKS):
                    last = pe.transpose(W1[0:EXPERTS, c * CT:(c + 1) * CT], gates[:, c], ident[0:CT, 0:CT])
                last.then_inc(gates_turned, 1)

            def e_start(n):
                pe.wait_ge(gates_split_ready, n + 1)
                for s in range(2):
                    mm(moe_ps[:, 0:BT], b2_w[s][:], gates_split[:], start=(s == 0), stop=False,
                       skip_group_check=True)

            def e_up(n, e):
                if e >= 2:
                    pe.wait_ge(hidden_ready, EXPERTS * n + e - 1)
                    pe.wait_ge(gated_ready, EXPERTS * n + e - 1)
                for s in range(2):
                    last = mm(up_ps[e % 2][:, 0:BT], up_w[s][:, e], x2_split[:], start=(s == 0), stop=(s == 1))
                last.then_inc(up_done, 1)
                mm(gate_ps[e % 2][:, 0:BT], sel[:, e], gates_split[:], start=True, stop=True).then_inc(gate_done, 1)

            def e_down(n, e):
                pe.wait_ge(gated_ready, EXPERTS * n + e + 1)
                half = 64 * (e % 2)
                mm(moe_ps[half:half + 64, 0:BT], down_w[:, e], gated[:, e % 2], start=False,
                   stop=(e >= EXPERTS - 2), skip_group_check=True).then_inc(down_done, 1)

            def e_fold(n):
                pe.wait_ge(moe_copied, n + 1)
                for c in range(CHUNKS):
                    last = mm(moe_ps[0:CT, c * EMB:(c + 1) * EMB], moe_sb[:, c * CT:(c + 1) * CT], fold[:],
                              start=True, stop=True)
                last.then_inc(moe_folded, 1)

            def retention(n, rows, step):
                if step == 7: r_turn(xn, W0, n, xn_ready, n + 1, xn_turned)
                if step == 8: r_project(n)
                if step == 9: r_scores(n)
                if step == 10: r_state(n, rows)
                if step == 11: r_output(n)
                if step == 13: r_turn(x2, W2, n, x2_ready, n + 1, x2_turned)

            def tail(n):
                r_gate(n)
                r_turn_gates(n)

            pe.wait_ge(setup, N_SETUP)
            pe.wait_ge(loaded, N_LOADED)
            pe.wait_ge(filled, N_FILLED)
            for step in range(16):
                retention(0, 1, step)
            tail(0)
            with pe.Fori(0, IMAGES) as im:
                with pe.Fori(0, BLOCKS) as r:
                    it = im * BLOCKS + r
                    n = it + 1
                    e_start(it)
                    for e in range(EXPERTS):
                        e_up(it, e)
                        if e:
                            e_down(it, e - 1)
                        if e == 0:
                            w_project_qk(it, n)
                            w_project_v(it, n)
                        if e == 1:
                            w_scores(it, n)
                        if e == 2:
                            w_spread_v(it, 0)
                            w_spread_v(it, 1)
                        if e == 3:
                            w_spread_v(it, 2)
                            w_spread_v(it, 3)
                        if e == 4: w_turn_probs(it)
                        if e == 5: w_values(it)
                        if e == 6: w_project_out(it)
                        retention(n, CT, e)
                    e_down(it, EXPERTS - 1)
                    e_fold(it)
                    tail(n)
            e_start(ALL_BLOCKS)
            for e in range(EXPERTS):
                e_up(ALL_BLOCKS, e)
                if e:
                    e_down(ALL_BLOCKS, e - 1)
            e_down(ALL_BLOCKS, EXPERTS - 1)
            e_fold(ALL_BLOCKS)

        @block.scalar
        def _(act):
            A = act.activation

            def w_split(it):
                act.wait_ge(x_loaded, 32 * it + 32)
                A(x_split[:], x_in[:], ACT.Copy).then_inc(x_high, 1)

            def w_evac_qk(it):
                act.wait_ge(qk_done, it + 1)
                for odd in range(2):
                    rows = slice(64 * odd, 64 * odd + 64)
                    A(q_zero[rows, :, odd, :], W0[rows, 0:HALF].rearrange("p (w q) -> p w q", q=QUERIES),
                      ACT.Identity, bias=q_bias[rows, 0:1], scale=float(HD) ** -0.5).then_inc(q_ready, 1)
                A(k_sb[:], W0[:, HALF:BT], ACT.Identity, bias=qk_bias[:, 1:2]).then_inc(k_copied, 1)

            def w_exp(it):
                act.wait_ge(shifted_ready, it + 1)
                A(probs[:], shifted[:], ACT.Exp).then_inc(exp_ready, 1)

            def w_evac_probs(it):
                act.wait_ge(probs_turned, it + 1)
                A(probs_t[:], W0[:], ACT.Copy).then_inc(probs_t_ready, 1)

            def w_evac_att(it):
                act.wait_ge(av_done, it + 1)
                for odd in range(2):
                    A(att_t[0:EMB, :].rearrange("p (a c b) -> p a c b", a=ROWS, b=WIN)[:, :, odd::2, :],
                      W1[64 * odd:64 * odd + 64, 0:BT].rearrange("p (a c b) -> p a c b", a=ROWS, b=WIN)[:, :, odd::2, :],
                      ACT.Copy).then_inc(att_t_ready, 1)

            def w_evac_h1(it, n):
                act.wait_ge(h1_done, it + 1)
                A(h1[:].rearrange("p c n -> p (c n)"), W2[0:CT, 0:256], ACT.Copy).then_inc(h1_ready, 1)

            def r_split(n):
                act.wait_ge(xn_turned, n + 1)
                A(xn_split[:], W0[:, 0:BT], ACT.Copy).then_inc(xn_high, 1)

            def r_evac_v(n):
                act.wait_ge(rv_done, n + 1)
                A(v2[:].rearrange("p c n -> p (c n)"), W0[0:CT, 0:256], ACT.Copy).then_inc(v2_ready, 1)

            def r_evac_k(n, variant):
                act.wait_ge(kt_turned, n + 1)
                A(k_dec[:].rearrange("p c n -> p (c n)"), W2[0:CT, 0:256], ACT.Copy,
                  scale=key_decay[:, variant:variant + 1]).then_inc(k_dec_ready, 1)

            def retention(n, variant, step):
                if step == 7: r_split(n)
                if step == 8: r_evac_v(n)
                if step == 9: r_evac_k(n, variant)

            def tail(n):
                act.wait_ge(x2_turned, n + 1)
                A(x2_split[:], W2[:, 0:BT], ACT.Copy).then_inc(x2_high, 1)
                act.wait_ge(diff_ready, n + 1)
                A(top_exp[:], top_diff[:], ACT.Exp).then_inc(gexp_ready, 1)
                act.wait_ge(gates_turned, n + 1)
                A(gates_split[0:EXPERTS, :], W1[0:EXPERTS, 0:BT], ACT.Copy).then_inc(gates_high, 1)

            def e_hidden(n, e):
                act.wait_ge(up_done, EXPERTS * n + e + 1)
                if e >= 2:
                    act.wait_ge(gated_ready, EXPERTS * n + e - 1)
                A(hidden[:, e % 2], up_ps[e % 2][:, 0:BT], ACT.Relu, bias=up_bias[:, e:e + 1]).then_inc(hidden_ready, 1)

            def e_copy(n):
                act.wait_ge(down_done, EXPERTS * n + EXPERTS)
                A(moe_sb[:], moe_ps[:, 0:BT], ACT.Copy).then_inc(moe_copied, 1)

            act.wait_ge(setup, N_SETUP)
            act.wait_ge(loaded, N_LOADED)
            act.wait_ge(filled, N_FILLED)
            for step in range(16):
                retention(0, 1, step)
            tail(0)
            with act.Fori(0, IMAGES) as im:
                with act.Fori(0, BLOCKS) as r:
                    it = im * BLOCKS + r
                    n = it + 1
                    w_split(it)
                    for e in range(EXPERTS):
                        e_hidden(it, e)
                        if e == 0: w_evac_qk(it)
                        if e == 2: w_exp(it)
                        if e == 4: w_evac_probs(it)
                        if e == 5: w_evac_att(it)
                        if e == 6: w_evac_h1(it, n)
                        retention(n, 0, e)
                    e_copy(it)
                    tail(n)
            for e in range(EXPERTS):
                e_hidden(ALL_BLOCKS, e)
            e_copy(ALL_BLOCKS)

        @block.vector
        def _(dve):
            TT, TS, CP = dve.tensor_tensor, dve.tensor_scalar, dve.tensor_copy

            made = [0]

            def did(ins):
                made[0] += 1
                ins.then_inc(setup, 1)

            def settle():
                dve.wait_ge(setup, made[0])

            dve.wait_ge(loaded, N_LOADED)
            dve.wait_ge(filled, N_FILLED)
            for odd in range(2):
                cols = slice(64 * odd, 64 * odd + 64)
                did(CP(q_even_odd[odd][0][:, cols], qk_raw[:, 0]))
                did(CP(k_even_odd[odd][0][:, cols], qk_raw[:, 1]))
            did(CP(v_w[0][:], v_raw[:]))
            did(CP(r_w[0][:], r_raw[:]))
            did(CP(gate_w[0][:], gate_raw[:]))
            did(CP(up_w[0][:], up_raw[:]))
            did(CP(b2_w[0][:], b2_raw[:]))
            settle()
            for odd in range(2):
                cols = slice(64 * odd, 64 * odd + 64)
                did(TT(q_even_odd[odd][1][:, cols], qk_raw[:, 0], q_even_odd[odd][0][:, cols].bitcast(F32), ALU.subtract))
                did(TT(k_even_odd[odd][1][:, cols], qk_raw[:, 1], k_even_odd[odd][0][:, cols].bitcast(F32), ALU.subtract))
            did(TT(v_w[1][:], v_raw[:], v_w[0][:].bitcast(F32), ALU.subtract))
            did(TT(r_w[1][:], r_raw[:], r_w[0][:].bitcast(F32), ALU.subtract))
            did(TT(gate_w[1][:], gate_raw[:], gate_w[0][:].bitcast(F32), ALU.subtract))
            did(TT(up_w[1][:], up_raw[:], up_w[0][:].bitcast(F32), ALU.subtract))
            did(TT(b2_w[1][:], b2_raw[:], b2_w[0][:].bitcast(F32), ALU.subtract))
            did(CP(sel[:], broadcast(sel_row[:], 2, 128)))
            wb = win_bias[:].rearrange("p a b q -> p (a b) q")
            did(TT(wb, wb, broadcast(pos_bias[:], 1, BLOCKS * 4), ALU.add))
            did(dve.memset(att_t[EMB:EMB + 1, :], 1.0))
            did(TS(q_bias[:], qk_bias[:, 0:1], float(HD) ** -0.5, None, ALU.mult))
            assert made[0] == N_SETUP
            settle()

            def w_split(it):
                dve.wait_ge(x_high, it + 1)
                TT(x_split[64:128, :], x_in[64:128, :], x_split[64:128, :].bitcast(F32), ALU.subtract).then_inc(x_ready, 1)

            def w_evac_v(it):
                dve.wait_ge(v_done, it + 1)
                TT(v_tok[:], W1[0:CT, 0:256].rearrange("p (t n) -> p t n", n=EMB), broadcast(v_bias[:], 1, 4),
                   ALU.add).then_inc(v_ready, 1)

            def w_softmax(it, r):
                ch = link(dve, chain1, it, CH1)
                dve.wait_ge(s_done, it + 1)
                bias = win_bias[:, bass.ds(r, 1)].rearrange("p o g q -> p (o g) q")
                ch(TT(logits[:], W2[:].rearrange("p (g h q) -> p g h q", g=4, h=HEADS), broadcast(bias, 2, HEADS), ALU.add))
                ch(dve.tensor_reduce(row_max[:], logits[:], AX.X, ALU.max))
                TT(shifted[:], logits[:], broadcast(row_max[:], 3, QUERIES), ALU.subtract).then_inc(shifted_ready, 1)
                return ch

            def w_normalise(it, ch):
                dve.wait_ge(exp_ready, it + 1)
                ch(dve.tensor_reduce(row_sum[:], probs[:], AX.X, ALU.add))
                ch(dve.reciprocal(row_inv[:], row_sum[:]))
                TT(probs_n[:], probs[:], broadcast(row_inv[:], 3, QUERIES), ALU.mult).then_inc(probs_ready, 1)

            def w_mask_v(it, j):
                dve.wait_ge(v_spread, 4 * it + j + 1)
                W = (W1, W2)[j % 2]
                m = min(2, WPT - 2 * j)
                TT(v_heads[:, 2 * j:2 * j + m].rearrange("p k t n -> p (k t) n"),
                   W[:, 0:256 * m].rearrange("p (a n) -> p a n", n=EMB),
                   broadcast(head_columns[:], 1, 4 * m), ALU.mult).then_inc(v_masked, 1)

            def norm_stats(src, st, mv, ch, ready):
                for c in range(CHUNKS):
                    ins = dve.bn_stats(st[:, c], src[:, c])
                ch(ins)
                TT(mv[:, :, 0], st[:, :, 1], st[:, :, 4], ALU.add)
                TT(mv[:, :, 1], st[:, :, 1], st[:, :, 4], ALU.subtract)
                ch(TT(mv[:, :, 2], st[:, :, 2], st[:, :, 5], ALU.add))
                ch(dve.scalar_tensor_tensor(mv[:, :, 3], mv[:, :, 1], 0.25, mv[:, :, 1], ALU.mult, ALU.mult))
                dve.scalar_tensor_tensor(mv[:, :, 4], mv[:, :, 2], 1.0 / EMB, mv[:, :, 3],
                                         ALU.mult, ALU.add).then_inc(ready, 1)

            def norm_apply(src, mv, rs, mid, dst, ch, ready, count, done):
                ch(dve.scalar_tensor_tensor(mid[:], mv[:, :, 0:1].broadcast_to([CT, CHUNKS, EMB]), -0.5, src[:],
                                            ALU.mult, ALU.add))
                dve.wait_ge(ready, count)
                if len(dst.shape) == 4:
                    ins = TT(dst[:], broadcast(mid[:], 2, 2), broadcast(broadcast(rs[:], 2, 2), 3, EMB), ALU.mult)
                else:
                    ins = TT(dst[:], mid[:], broadcast(rs[:], 2, EMB), ALU.mult)
                ins.then_inc(done, 1)

            def r_norm1(n, ch, first):
                if not first:
                    dve.wait_ge(h1_ready, n)
                norm_stats(h1, stats, mean_var, ch, var_ready)
                norm_apply(h1, mean_var, rstd, centred, xn, ch, rstd_ready, 2 * n + 1, xn_ready)

            def r_split(n):
                dve.wait_ge(xn_high, n + 1)
                TT(xn_split[64:128, :], W0[64:128, 0:BT], xn_split[64:128, :].bitcast(F32),
                   ALU.subtract).then_inc(xn_split_ready, 1)

            def r_rotate(n, ch, cos, sin):
                dve.wait_ge(rqk_done, n + 1)
                TT(rot_cos[:], W1[:, 0:BT], cos, ALU.mult)
                ch(TT(rot_sin[:], W2[:, 0:BT], sin, ALU.mult))
                TT(q_t[:], rot_cos[0:64, :], rot_sin[0:64, :], ALU.add)
                TT(k_t[:], rot_cos[64:128, :], rot_sin[64:128, :], ALU.add).then_inc(rot_ready, 1)

            def r_decay(n, variant):
                dve.wait_ge(kq_done, n + 1)
                TT(att[:], W1[0:CT, 0:BT].rearrange("p (c n) -> p c n", n=CT),
                   broadcast(decay[:, variant], 1, CHUNKS), ALU.mult).then_inc(att_ready, 1)

            def r_state(it, n):
                ch = link(dve, chain_s, it, CHS)
                ch(CP(state[:, 0], state[:, CHUNKS]))
                dve.wait_ge(state_done, n + 1)
                for c in range(CHUNKS):
                    ins = dve.scalar_tensor_tensor(state[:, c + 1], state[:, c], GAMMA ** CT,
                                                   W0[0:EMB, c * EMB:(c + 1) * EMB], ALU.mult, ALU.add)
                    if c < CHUNKS - 1:
                        ch(ins)
                ins.then_inc(state_ready, 1)

            def r_residual(n, ch, first=False):
                dve.wait_ge(ret_done, n + 1)
                ch(TT(h1_intra[:].rearrange("p c n -> p (c n)"), W1[0:CT, 0:256], h1[:].rearrange("p c n -> p (c n)"), ALU.add))
                if not first:
                    dve.wait_ge(kept, n)
                dve.scalar_tensor_tensor(h2[:].rearrange("p c n -> p (c n)"), W1[0:CT, 256:512], query_decay[:, 0:1],
                                         h1_intra[:].rearrange("p c n -> p (c n)"), ALU.mult, ALU.add).then_inc(h2_ready, 1)

            def r_norm2(n, ch):
                dve.wait_ge(h2_ready, n + 1)
                norm_stats(h2, stats, mean_var, ch, var_ready)
                norm_apply(h2, mean_var, rstd, centred, x2, ch, rstd_ready, 2 * n + 2, x2_ready)

            def tail(n, ch):
                dve.wait_ge(x2_high, n + 1)
                TT(x2_split[64:128, :], W2[64:128, 0:BT], x2_split[64:128, :].bitcast(F32),
                   ALU.subtract).then_inc(x2_split_ready, 1)
                dve.wait_ge(gl_done, n + 1)
                ins = TT(gate_logits[:], W0[0:CT, 0:CHUNKS * EXPERTS].rearrange("p (c e) -> p c e", e=EXPERTS),
                         broadcast(gate_bias[:], 1, CHUNKS), ALU.add)
                ins.then_inc(gl_ready, 1)
                dve.wait_ge(gl_ready, n + 1)
                CP(x2_keep[:], x2[:, :, 0])
                for c in range(CHUNKS):
                    ins = dve.max(top_val[:, c], gate_logits[:, c])
                ch(ins)
                TT(top_diff[:], top_val[:, :, 1], top_val[:, :, 0], ALU.subtract).then_inc(diff_ready, 1)
                for c in range(CHUNKS):
                    ins = dve.max_index(top_idx[:, c], top_val[:, c], gate_logits[:, c])
                ch(ins)
                ch(CP(top_id[:], top_idx[:, :, 0:2]))
                for k in range(TOP):
                    ins = TT(one_hot[:, k], broadcast(expert_ids[:], 1, CHUNKS),
                             top_id[:, :, k:k + 1].broadcast_to([CT, CHUNKS, EXPERTS]), ALU.is_equal)
                ch(ins)
                dve.wait_ge(gexp_ready, n + 1)
                ch(TS(top_den[:], top_exp[:], 1.0, None, ALU.add))
                ch(dve.reciprocal(top_w[:, 0], top_den[:]))
                ch(TT(top_w[:, 1], top_w[:, 0], top_exp[:], ALU.mult))
                for k in range(TOP):
                    ins = TT(gates_a[:, k], one_hot[:, k], broadcast(top_w[:, k], 2, EXPERTS), ALU.mult)
                ch(ins)
                TT(gates[:], gates_a[:, 0], gates_a[:, 1], ALU.add).then_inc(gates_ready, 1)
                dve.wait_ge(gates_high, n + 1)
                TT(gates_split[32:32 + EXPERTS, :], W1[0:EXPERTS, 0:BT], gates_split[0:EXPERTS, :].bitcast(F32),
                   ALU.subtract).then_inc(gates_split_ready, 1)

            def e_gate(n, e):
                dve.wait_ge(hidden_ready, EXPERTS * n + e + 1)
                dve.wait_ge(gate_done, EXPERTS * n + e + 1)
                if e >= 2:
                    dve.wait_ge(down_done, EXPERTS * n + e - 1)
                TT(gated[:, e % 2], gate_ps[e % 2][:, 0:BT], hidden[:, e % 2], ALU.mult).then_inc(gated_ready, 1)

            def e_finish(n):
                ch = link(dve, chain3, n, CH3)
                dve.wait_ge(moe_folded, n + 1)
                ch(TT(res[:].rearrange("p c n -> p (c n)"), moe_ps[0:CT, 0:256],
                      x2_keep[:].rearrange("p c n -> p (c n)"), ALU.add))
                norm_stats(res, stats3, mean_var3, ch, var3_ready)
                norm_apply(res, mean_var3, rstd3, centred3, normed3, ch, rstd3_ready, n + 1, normed3_ready)

            ch = link(dve, chain2, 0, CH2)
            r_norm1(0, ch, True)
            r_split(0)
            r_rotate(0, ch, cls_cos[:], cls_sin[:])
            r_decay(0, 1)
            dve.wait_ge(state_done, 1)
            CP(state_cls[:], W0[0:EMB, 0:EMB]).then_inc(state_ready, 1)
            r_residual(0, ch, True)
            r_norm2(0, ch)
            tail(0, ch)
            with dve.Fori(0, IMAGES) as im:
                CP(state[:, CHUNKS], state_cls[:])
                with dve.Fori(0, BLOCKS) as r:
                    it = im * BLOCKS + r
                    n = it + 1
                    ch = link(dve, chain2, n, CH2)
                    w_split(it)
                    for e in range(EXPERTS):
                        e_gate(it, e)
                        if e == 0: w_evac_v(it)
                        if e == 1: ch1 = w_softmax(it, r)
                        if e == 2:
                            w_mask_v(it, 0)
                            w_mask_v(it, 1)
                            w_normalise(it, ch1)
                        if e == 3:
                            w_mask_v(it, 2)
                            w_mask_v(it, 3)
                        if e == 6: r_norm1(n, ch, False)
                        if e == 7: r_split(n)
                        if e == 8: r_rotate(n, ch, cos_t[:, bass.ds(r * BT + 1, BT)], sin_t[:, bass.ds(r * BT + 1, BT)])
                        if e == 9: r_decay(n, 0)
                        if e == 10: r_state(it, n)
                        if e == 11: r_residual(n, ch)
                        if e == 12: r_norm2(n, ch)
                    e_finish(it)
                    tail(n, ch)
            for e in range(EXPERTS):
                e_gate(ALL_BLOCKS, e)
            e_finish(ALL_BLOCKS)

        @block.gpsimd
        def _(pool):
            TT = pool.tensor_tensor

            cleared = [q_even_odd[0][0], q_even_odd[0][1], q_even_odd[1][0], q_even_odd[1][1],
                       k_even_odd[0][0], k_even_odd[0][1], k_even_odd[1][0], k_even_odd[1][1]]
            for t in cleared:
                pool.memset(t[:].bitcast(F32), 0.0)
            pool.memset(b2_raw[:], 0.0)
            pool.memset(gates_split[:].bitcast(F32), 0.0)
            pool.memset(q_zero[:], 0.0).then_inc(filled, 1)
            pool.memset(state[:], 0.0).then_inc(filled, 1)
            pool.memset(cls_cos[:], 1.0).then_inc(filled, 1)
            pool.memset(cls_sin[:], 0.0).then_inc(filled, 1)
            pool.memset(eps_t[:], EPS)
            pool.memset(power[:], -0.5).then_inc(filled, 1)
            pool.memset(h3[:], 0.0).then_inc(stored, 16)

            def w_expand_k(it):
                pool.wait_ge(k_copied, it + 1)
                pool.tensor_tensor(
                    k_heads[:], broadcast(k_sb[:].rearrange("p (w q) -> p w q", q=QUERIES), 2, HEADS),
                    broadcast(broadcast(head_of_channel[:], 1, PAIRS), 3, QUERIES), ALU.mult).then_inc(k_ready, 1)

            def inverse_root(mv, ve, rs, ch, ready, count, done):
                pool.wait_ge(ready, count)
                ch(TT(ve[:], mv[:, :, 4], eps_t[:], ALU.add))
                TT(rs[:], ve[:], power[:], ALU.pow).then_inc(done, 1)

            def keep(n, first=False):
                pool.wait_ge(x2_ready, n + 1)
                if not first:
                    pool.wait_ge(h3_ready, n)
                TT(h2_keep[:], h2[:], broadcast(ln_beta[:], 1, CHUNKS), ALU.add).then_inc(kept, 1)

            def e_finish(n, ch):
                inverse_root(mean_var3, var_eps3, rstd3, ch, var3_ready, n + 1, rstd3_ready)
                pool.wait_ge(normed3_ready, n + 1)
                pool.wait_ge(stored, 16 * n + 16)
                ch(TT(h3[:], normed3[:], broadcast(ln_gamma[:], 1, CHUNKS), ALU.mult))
                TT(h3[:], h3[:], h2_keep[:], ALU.add).then_inc(h3_ready, 1)

            pool.wait_ge(loaded, N_LOADED)
            pool.wait_ge(filled, N_FILLED)
            ch = link(pool, pool_chain2, 0, CHP2)
            inverse_root(mean_var, var_eps, rstd, ch, var_ready, 1, rstd_ready)
            inverse_root(mean_var, var_eps, rstd, ch, var_ready, 2, rstd_ready)
            keep(0, True)
            with pool.Fori(0, ALL_BLOCKS) as it:
                n = it + 1
                w_expand_k(it)
                ch = link(pool, pool_chain2, n, CHP2)
                inverse_root(mean_var, var_eps, rstd, ch, var_ready, 2 * n + 1, rstd_ready)
                inverse_root(mean_var, var_eps, rstd, ch, var_ready, 2 * n + 2, rstd_ready)
                e_finish(it, link(pool, pool_chain3, it, CHP3))
                keep(n)
            e_finish(ALL_BLOCKS, link(pool, pool_chain3, ALL_BLOCKS, CHP3))


def constants():
    t = {}
    p = np.arange(128)
    f = np.float32
    rows = np.zeros((QUERIES, QUERIES))
    s = WIN * (WIN // 2)
    rows[-s:, :-s] = MASKED
    rows[:-s, -s:] = MASKED
    cols = rows.reshape(WIN, WIN, WIN, WIN).transpose(1, 0, 3, 2).reshape(QUERIES, QUERIES)
    mask = np.zeros((4, 2, QUERIES, BLOCKS, 4, QUERIES), f)
    for pair in range(PAIRS):
        g, c = divmod(pair, 4)
        wr, k = divmod(pair, WPT)
        if wr == 1:
            mask[c, :, :, BLOCKS - 1, g, :] += rows
        if k == WPT - 1:
            mask[c, 1, :, :, g, :] += cols[:, None, :]
    t["win_mask"] = mask.reshape(128, -1)
    t["head_of_channel"] = ((p[:, None] % EMB) // HD == np.arange(HEADS)).astype(f)
    t["head_columns"] = (p[:, None] // QUERIES == np.arange(EMB) // HD).astype(f)
    q = np.arange(CT)
    t["pick"] = ((q[:, None, None] // QUERIES == np.arange(WPT)[:, None]) &
                 (q[:, None, None] % QUERIES == p % QUERIES)).astype(f).reshape(CT, -1)
    t["ident"] = np.eye(128, dtype=f)
    inv = f(1.0) / np.power(f(THETA), np.arange(0, EMB, 2, dtype=f) / f(EMB), dtype=f)
    angle = np.arange(SEQ, dtype=f)[:, None] * inv[None, :]
    cos, sin = np.cos(angle).astype(f), np.sin(angle).astype(f)
    t["cos"] = np.tile(np.repeat(cos, 2, axis=1).T, (2, 1)).astype(f)
    t["sin"] = np.tile(np.stack([-sin, sin], axis=2).reshape(SEQ, EMB).T, (2, 1)).astype(f)
    n = np.arange(CT)
    diff = n[None, :] - n[:, None]
    within = np.where(diff >= 0, GAMMA ** np.maximum(diff, 0).astype(np.float64), 0.0)
    t["decay"] = np.stack([within, np.eye(CT)], axis=1).astype(f).reshape(CT, -1)
    t["key_decay"] = np.stack([GAMMA ** (CT - 1.0 - n), np.ones(CT)], axis=1).astype(f)
    t["query_decay"] = (GAMMA ** (n + 1.0))[:, None].astype(f)
    t["expert_ids"] = np.tile(np.arange(EXPERTS, dtype=f), (CT, 1))
    e = np.arange(EXPERTS)
    t["sel_row"] = ((p[:, None] == e) | (p[:, None] == 32 + e)).astype(f)
    t["fold"] = np.tile(np.eye(EMB, dtype=f), (2, 1))
    return {k: np.ascontiguousarray(v) for k, v in t.items()}


def lay_out(d):
    a = {}
    x = np.roll(d["x"], (-(WIN // 2), -(WIN // 2)), axis=(2, 3))
    x = x.reshape(IMAGES, EMB, BLOCKS, 2, WIN, WPT, 2, WIN)
    a["x"] = x.transpose(0, 2, 1, 6, 3, 5, 4, 7).reshape(ALL_BLOCKS, EMB, BT)
    w1 = d["L0_tok_w1"].reshape(HD, HEADS, 3, EMB).transpose(2, 3, 1, 0).reshape(3, EMB, EMB)
    b1 = d["L0_tok_b1"].reshape(HD, HEADS, 3).transpose(2, 1, 0).reshape(3, EMB)
    a["w_qk"] = w1[0:2].transpose(1, 0, 2)
    a["w_v"] = w1[2]
    a["b_qk"] = b1[0:2].T
    a["b_v"] = np.tile(b1[2], (CT, 1))
    a["w_out"] = np.concatenate([d["L0_tok_w2"].T, d["L0_tok_b2"][None]], axis=0)
    c = np.array([[i, j] for i in range(WIN) for j in range(WIN)])
    rel = c[None, :, :] - c[:, None, :] + WIN - 1
    a["pos"] = np.tile(d["L0_tok_pos_emb"][rel[..., 0], rel[..., 1]], (128 // QUERIES, 1))
    swap = np.arange(EMB) ^ 1
    wq, wk = d["L0_attn_W_Q"], d["L0_attn_W_K"]
    a["w_ret"] = np.stack([wq, wk, wq[:, swap], wk[:, swap], d["L0_attn_W_V"]], axis=1)
    a["w_gate"] = d["L0_ffn_gate_w"]
    a["b_gate"] = np.tile(d["L0_ffn_gate_b"], (CT, 1))
    a["w_up"] = d["L0_ffn_w1"].transpose(1, 0, 2)
    a["b_up"] = d["L0_ffn_b1"].T
    a["w_down"] = d["L0_ffn_w2"].transpose(1, 0, 2)
    a["b_down"] = d["L0_ffn_b2"]
    a["gamma"] = np.tile(d["L0_ffn_gamma"], (CT, 1))
    a["beta"] = np.tile(d["L0_ffn_beta"], (CT, 1))
    a["cls"] = np.tile(d["cls_tok"].reshape(1, EMB), (CT, CHUNKS))
    return {k: np.ascontiguousarray(v) for k, v in a.items()}


def kernel(**inputs):
    import concourse.bacc as bacc
    from concourse.bass_utils import run_bass_kernel_spmd

    arrays = lay_out({k: np.asarray(v) for k, v in inputs.items()})
    arrays.update(constants())
    nc = bacc.Bacc("TRN2", target_bir_lowering=False, num_devices=1)
    aps = {k: nc.dram_tensor("in_" + k, v.shape, mybir.dt.from_np(v.dtype), kind="ExternalInput").ap()
           for k, v in arrays.items()}
    out = nc.dram_tensor("out_y", ((ALL_BLOCKS + 1) * CHUNKS, CT, EMB), F32, kind="ExternalOutput").ap()
    build_tower(nc, aps, out)
    r = run_bass_kernel_spmd(nc, [{"in_" + k: v for k, v in arrays.items()}], core_ids=[0])
    got = np.asarray(r.results[0]["out_y"])
    cls = np.tile(got[0, 0].reshape(1, 1, EMB), (IMAGES, 1, 1))
    return np.concatenate([cls, got[CHUNKS:].reshape(IMAGES, SIDE * SIDE, EMB)], axis=1)
```

```python
from contextlib import ExitStack

import numpy as np

import concourse.bass as bass
from concourse import mybir

F32 = mybir.dt.float32
F32R = mybir.dt.float32r
U32 = mybir.dt.uint32
ALU = mybir.AluOpType
ACT = mybir.ActivationFunctionType
AX = mybir.AxisListType

IMAGES, EMB, SIDE = 4, 64, 56
HEADS, WIN, HD = 8, 4, 8
EXPERTS, FF, TOP = 16, 128, 2
GAMMA, THETA, EPS = 0.96875, 10000.0, 1e-5
QUERIES = WIN * WIN
ROWS = 2 * WIN
BT = ROWS * SIDE
BLOCKS = SIDE // ROWS
ALL_BLOCKS = IMAGES * BLOCKS
CT = 2 * SIDE
CHUNKS = BT // CT
PAIRS = BT // QUERIES // 2
WPT = CT // QUERIES
HALF = BT // 2
SEQ = 1 + SIDE * SIDE
MASKED = -1e30
HIDDEN_BUFS, GATED_BUFS = 4, 8

LOOP_FROM = 2

PE_AT = dict(qk=1, v=1, spread=(3, 4, 6, 7), scores=5, probs=9, values=10, out=12,
             xn=0, rqk=2, rscores=4, rv=4, state=6, output=8, x2=11, logits=13, gates=15,
             open=21, fold=35, ahead=0)
ACT_AT = dict(x=0, qk=1, exp=6, probs=9, values=10, out=12,
              xn=0, kv=4, x2=11, exp_gate=13, gates=15, copy=34)
DVE_AT = dict(x=0, v=1, mask=(3, 4, 6, 7), softmax=5, normalise=7,
              stats1=-3, norm1=-2, xn=0, rotate=2, decay=4, state=6, residual=8, stats2=8, norm2=9,
              x2=11, top=13, gates=14, gates_low=15, added=35, norm3=37)
POOL_AT = dict(keys=1, root1=-3, root2=8, root3=35, finish=38)
EXPERT_AT = 16
DOWN_LAG = 2


def later(n):
    return not isinstance(n, int) or n > 0


def broadcast(ap, axis, n):
    ap = ap.unsqueeze(axis)
    shape = list(ap.shape)
    shape[axis] = n
    return ap.broadcast_to(shape)


def build_tower(nc, I, y):
    ctx = ExitStack()
    with ctx:
        def sb(name, shape, dt=F32):
            return ctx.enter_context(nc.sbuf_tensor(name, shape, dt))

        def ps(name, shape):
            return ctx.enter_context(nc.psum_tensor(name, shape, F32))

        def sem(name):
            return ctx.enter_context(nc.semaphore(name))

        qk_raw = sb("qk_raw", [128, 2, EMB])
        q_even_odd = [[sb(f"q_w{p}{s}", [128, 128], F32R) for s in "hl"] for p in "eo"]
        k_even_odd = [[sb(f"k_w{p}{s}", [128, 128], F32R) for s in "hl"] for p in "eo"]
        v_raw = sb("v_raw", [128, EMB])
        v_w = [sb(f"v_w{s}", [128, EMB], F32R) for s in "hl"]
        qk_bias = sb("qk_bias", [128, 2])
        q_bias = sb("q_bias", [128, 1])
        v_bias = sb("v_bias", [CT, EMB])
        out_w = sb("out_w", [EMB + 1, EMB])
        win_bias = sb("win_bias", [128, ALL_BLOCKS, 4, QUERIES])
        pos_bias = sb("pos_bias", [128, QUERIES])
        head_of_channel = sb("head_of_channel", [128, HEADS])
        head_columns = sb("head_columns", [128, EMB])
        pick = sb("pick", [CT, WPT, 128])
        ident = sb("ident", [128, 128])
        r_raw = sb("r_raw", [128, 5, EMB])
        r_w = [sb(f"r_w{s}", [128, 5, EMB], F32R) for s in "hl"]
        cos_t = sb("cos_t", [128, 1 + SIDE * SIDE])
        sin_t = sb("sin_t", [128, 1 + SIDE * SIDE])
        cls_cos = sb("cls_cos", [128, BT])
        cls_sin = sb("cls_sin", [128, BT])
        decay = sb("decay", [CT, 2, CT])
        key_decay = sb("key_decay", [CT, 2])
        query_decay = sb("query_decay", [CT, 1])
        gate_raw = sb("gate_raw", [128, EXPERTS])
        gate_w = [sb(f"gate_w{s}", [128, EXPERTS], F32R) for s in "hl"]
        gate_bias = sb("gate_bias", [CT, EXPERTS])
        expert_ids = sb("expert_ids", [CT, EXPERTS])
        up_raw = sb("up_raw", [128, EXPERTS, FF])
        up_w = [sb(f"up_w{s}", [128, EXPERTS, FF], F32R) for s in "hl"]
        up_bias = sb("up_bias", [FF, EXPERTS])
        down_w = sb("down_w", [FF, EXPERTS, EMB])
        b2_raw = sb("b2_raw", [128, 128])
        b2_w = [sb(f"b2_w{s}", [128, 128], F32R) for s in "hl"]
        sel_row = sb("sel_row", [128, EXPERTS])
        sel = sb("sel", [128, EXPERTS, 128], F32R)
        fold = sb("fold", [128, EMB])
        ln_gamma = sb("ln_gamma", [CT, EMB])
        ln_beta = sb("ln_beta", [CT, EMB])
        power = sb("power", [CT, CHUNKS])
        eps_t = sb("eps_t", [CT, CHUNKS])

        x_in = sb("x_in", [128, BT])
        x_split = sb("x_split", [128, BT], F32R)
        k_sb = sb("k_sb", [128, HALF])
        q_zero = sb("q_zero", [128, PAIRS, 2, QUERIES])
        k_heads = sb("k_heads", [128, PAIRS, HEADS, QUERIES])
        v_tok = sb("v_tok", [CT, 4, EMB])
        v_heads = sb("v_heads", [128, WPT, 4, EMB])
        logits = sb("logits", [128, 4, HEADS, QUERIES])
        shifted = sb("shifted", [128, 4, HEADS, QUERIES])
        probs = sb("probs", [128, 4, HEADS, QUERIES])
        probs_n = sb("probs_n", [128, 4, HEADS, QUERIES])
        row_max = sb("row_max", [128, 4, HEADS])
        row_sum = sb("row_sum", [128, 4, HEADS])
        row_inv = sb("row_inv", [128, 4, HEADS])
        probs_t = sb("probs_t", [128, BT + 64])
        att_t = sb("att_t", [EMB + 1, BT])
        h1 = [sb(f"h1_{i}", [CT, CHUNKS, EMB]) for i in range(2)]
        xn = sb("xn", [CT, CHUNKS, 2, EMB])
        stats, mean_var, var_eps, rstd, centred = (
            [sb(f"{name}{k}", shape) for k in range(3)]
            for name, shape in (("stats", [CT, CHUNKS, 6]), ("mean_var", [CT, CHUNKS, 5]), ("var_eps", [CT, CHUNKS]),
                                ("rstd", [CT, CHUNKS]), ("centred", [CT, CHUNKS, EMB])))
        xn_split = sb("xn_split", [128, BT], F32R)
        rot_cos = sb("rot_cos", [128, BT])
        rot_sin = sb("rot_sin", [128, BT])
        q_t = sb("q_t", [EMB, BT])
        k_t = sb("k_t", [EMB, BT])
        v2 = sb("v2", [CT, CHUNKS, EMB])
        att = sb("att", [CT, CHUNKS, CT])
        k_dec = sb("k_dec", [CT, CHUNKS, EMB])
        state = sb("state", [EMB, CHUNKS + 1, EMB])
        state_cls = sb("state_cls", [EMB, EMB])
        state_mid = sb("state_mid", [EMB, EMB])
        carry = sb("carry", [EMB, 2, ALL_BLOCKS + 1])
        h1_intra = sb("h1_intra", [CT, CHUNKS, EMB])
        h2 = [sb(f"h2_{i}", [CT, CHUNKS, EMB]) for i in range(2)]
        x2 = [sb(f"x2_{i}", [CT, CHUNKS, 2, EMB]) for i in range(2)]
        gate_logits = sb("gate_logits", [CT, CHUNKS, EXPERTS])
        top_sum = sb("top_sum", [CT, CHUNKS])
        top_val = sb("top_val", [CT, CHUNKS, 8])
        top_idx = sb("top_idx", [CT, CHUNKS, 8], U32)
        top_id = sb("top_id", [CT, CHUNKS, 2])
        top_diff = sb("top_diff", [CT, CHUNKS])
        top_exp = sb("top_exp", [CT, CHUNKS])
        top_den = sb("top_den", [CT, CHUNKS])
        top_w = sb("top_w", [CT, 2, CHUNKS])
        one_hot = sb("one_hot", [CT, 2, CHUNKS, EXPERTS])
        gates_a = sb("gates_a", [CT, 2, CHUNKS, EXPERTS])
        gates = sb("gates", [CT, CHUNKS, EXPERTS])
        x2_split = [sb(f"x2_split{i}", [128, BT], F32R) for i in range(2)]
        gates_split = [sb(f"gates_split{i}", [128, BT], F32R) for i in range(2)]
        hidden = sb("hidden", [128, HIDDEN_BUFS, BT])
        gated = sb("gated", [128, GATED_BUFS, BT])
        moe_sb = sb("moe_sb", [128, BT])
        res = sb("res", [CT, CHUNKS, EMB])
        normed3 = sb("normed3", [CT, CHUNKS, EMB])
        h3 = sb("h3", [CT, CHUNKS, EMB])

        A0, A1 = (ps(f"win{i}", [128, 512]) for i in range(2))
        B0, B1 = (ps(f"ret{i}", [128, 512]) for i in range(2))
        up_ps = [ps(f"up{i}", [128, 512]) for i in range(2)]
        gate_ps = ps("gate", [128, 512])
        moe_ps = ps("moe", [128, 512])

        loaded = sem("loaded")
        filled = sem("filled")
        setup = sem("setup")
        x_loaded = sem("x_loaded")
        x_high = sem("x_high")
        x_ready = sem("x_ready")
        qk_done = sem("qk_done")
        v_done = sem("v_done")
        q_ready = sem("q_ready")
        k_copied = sem("k_copied")
        k_ready = sem("k_ready")
        v_ready = sem("v_ready")
        s_done = sem("s_done")
        chain1 = sem("chain1")
        chain_sums = sem("chain_sums")
        shifted_ready = sem("shifted_ready")
        exp_ready = sem("exp_ready")
        probs_ready = sem("probs_ready")
        probs_turned = sem("probs_turned")
        probs_t_ready = sem("probs_t_ready")
        v_spread = sem("v_spread")
        v_masked = sem("v_masked")
        av_done = sem("av_done")
        att_t_ready = sem("att_t_ready")
        h1_done = sem("h1_done")
        h1_ready = sem("h1_ready")
        chain_rotate = sem("chain_rotate")
        chain_residual = sem("chain_residual")
        chain_top = sem("chain_top")
        chain_gates = sem("chain_gates")
        chain_stats, chain_apply, var_ready, pool_chain, rstd_ready = (
            [sem(f"{name}{k}") for k in range(3)]
            for name in ("chain_stats", "chain_apply", "var_ready", "pool_chain", "rstd_ready"))
        pool_finish = sem("pool_finish")
        xn_ready = sem("xn_ready")
        xn_turned = sem("xn_turned")
        xn_high = sem("xn_high")
        xn_split_ready = sem("xn_split_ready")
        rqk_done = sem("rqk_done")
        rv_done = sem("rv_done")
        v2_ready = sem("v2_ready")
        rot_ready = sem("rot_ready")
        kq_done = sem("kq_done")
        att_ready = sem("att_ready")
        k_dec_ready = sem("k_dec_ready")
        state_done = sem("state_done")
        state_ready = sem("state_ready")
        ret_done = sem("ret_done")
        h2_ready = sem("h2_ready")
        x2_ready = sem("x2_ready")
        x2_turned = sem("x2_turned")
        x2_high = sem("x2_high")
        x2_split_ready = sem("x2_split_ready")
        gl_done = sem("gl_done")
        gl_ready = sem("gl_ready")
        diff_ready = sem("diff_ready")
        gexp_ready = sem("gexp_ready")
        gates_ready = sem("gates_ready")
        gates_turned = sem("gates_turned")
        gates_high = sem("gates_high")
        gates_split_ready = sem("gates_split_ready")
        up_done = sem("up_done")
        gate_done = sem("gate_done")
        hidden_ready = sem("hidden_ready")
        gated_ready = sem("gated_ready")
        down_done = sem("down_done")
        moe_copied = sem("moe_copied")
        moe_folded = sem("moe_folded")
        moe_added = sem("moe_added")
        chain_s = sem("chain_s")
        normed3_ready = sem("normed3_ready")
        h3_ready = sem("h3_ready")
        stored = sem("stored")

        def due(s, odd, e, at, blocks):
            n = s - at // EXPERTS
            if at % EXPERTS == e and (not isinstance(s, int) or 0 <= n < blocks):
                yield n, (odd - at // EXPERTS) % 2

        def link(eng, s, n, per):
            count = [0]

            def wait_for(ins):
                count[0] += 1
                assert count[0] <= per
                ins.then_inc(s, 1)
                eng.wait_ge(s, n * per + count[0])
            return wait_for

        loads = []
        for dst, name in (
            (qk_raw[0:64], "w_qk"), (qk_raw[64:128], "w_qk"), (v_raw[0:64], "w_v"), (v_raw[64:128], "w_v"),
            (qk_bias[0:64], "b_qk"), (qk_bias[64:128], "b_qk"), (v_bias[:], "b_v"), (out_w[:], "w_out"),
            (win_bias[:].rearrange("p a b c -> p (a b c)"), "win_mask"), (pos_bias[:], "pos"),
            (head_of_channel[:], "head_of_channel"), (head_columns[:], "head_columns"),
            (pick[:].rearrange("p a b -> p (a b)"), "pick"), (ident[:], "ident"),
            (r_raw[0:64], "w_ret"), (r_raw[64:128], "w_ret"), (cos_t[:], "cos"), (sin_t[:], "sin"),
            (decay[:].rearrange("p a b -> p (a b)"), "decay"), (key_decay[:], "key_decay"),
            (query_decay[:], "query_decay"), (gate_raw[0:64], "w_gate"), (gate_raw[64:128], "w_gate"),
            (gate_bias[:], "b_gate"), (expert_ids[:], "expert_ids"),
            (up_raw[0:64], "w_up"), (up_raw[64:128], "w_up"), (up_bias[:], "b_up"), (down_w[:], "w_down"),
            (sel_row[:], "sel_row"), (fold[:], "fold"), (ln_gamma[:], "gamma"), (ln_beta[:], "beta"),
            (h1[0][:].rearrange("p c n -> p (c n)"), "cls"), (carry[:].rearrange("p a b -> p (a b)"), "carry"),
        ):
            loads.append((dst, I[name]))
        B2_LOADS = 2
        N_LOADED = 16 * (len(loads) + B2_LOADS)
        N_FILLED = 5
        N_SETUP = 22

        block = ctx.enter_context(nc.Block())

        @block.sync
        def _(sp):
            for dst, src in loads:
                sp.dma_start(dst, src).then_inc(loaded, 16)
            sp.wait_ge(filled, N_FILLED)
            for row in (0, 32):
                sp.dma_start(b2_raw[row:row + EXPERTS, 0:EMB], I["b_down"]).then_inc(loaded, 16)

            def load_x(it):
                for half in (0, 64):
                    sp.dma_start(x_in[half:half + 64, :],
                                 I["x"][bass.ds(it, 1)].rearrange("o c t -> (o c) t")).then_inc(x_loaded, 16)

            def store(n):
                sp.wait_ge(h3_ready, n + 1)
                sp.dma_start(y[bass.ds(n * CHUNKS, CHUNKS)].rearrange("c t n -> t c n"), h3[:]).then_inc(stored, 16)

            load_x(0)
            sp.wait_ge(x_ready, 1)
            load_x(1)
            with sp.Fori(1, ALL_BLOCKS - 1) as it:
                sp.wait_ge(x_ready, it + 1)
                load_x(it + 1)
                store(it - 1)
            for n in range(ALL_BLOCKS - 2, ALL_BLOCKS + 1):
                store(n)
            sp.wait_ge(stored, 16 * (ALL_BLOCKS + 2))

        @block.tensor
        def _(pe):
            mm = pe.matmul

            def w_project_qk(it):
                pe.wait_ge(x_ready, it + 1)
                if later(it):
                    pe.wait_ge(h1_ready, it)
                for out, w in ((A0[:, 0:HALF], q_even_odd), (A0[:, HALF:BT], k_even_odd)):
                    for k in range(4):
                        last = mm(out, w[k // 2][k % 2][:], x_split[:, (k // 2) * HALF:(k // 2 + 1) * HALF],
                                  start=(k == 0), stop=(k == 3))
                last.then_inc(qk_done, 1)

            def w_project_v(it):
                for t in range(4):
                    for s in range(2):
                        last = mm(A1[0:CT, t * EMB:(t + 1) * EMB], x_split[:, t * CT:(t + 1) * CT], v_w[s][:],
                                  start=(s == 0), stop=(s == 1))
                last.then_inc(v_done, 1)

            def w_scores(it):
                pe.wait_ge(q_ready, 2 * it + 2)
                pe.wait_ge(k_ready, it + 1)
                pe.wait_ge(v_masked, 4 * it + 2)
                for g in range(4):
                    for c in range(4):
                        p = 4 * g + c if 4 * g + c < PAIRS else 4 * g + c - 2
                        last = mm(A1[32 * c:32 * c + 32, g * 128:(g + 1) * 128],
                                  q_zero[:, p].rearrange("p w q -> p (w q)"),
                                  k_heads[:, p].rearrange("p h q -> p (h q)"), start=True, stop=True)
                last.then_inc(s_done, 1)

            def w_spread_v(it, j):
                if j < 2:
                    pe.wait_ge(v_ready, it + 1)
                if j == 0:
                    pe.wait_ge(k_copied, it + 1)
                    pe.wait_ge(q_ready, 2 * it + 2)
                if j == 2:
                    pe.wait_ge(v_masked, 4 * it + 1)
                if j == 3:
                    pe.wait_ge(chain1, 2 * it + 1)
                bank = (A0, A1)[j % 2]
                for k in range(2 * j, min(2 * j + 2, WPT)):
                    last = mm(bank[:, (k % 2) * 256:(k % 2) * 256 + 256], pick[:, k, :],
                              v_tok[:].rearrange("p t n -> p (t n)"), start=True, stop=True)
                last.then_inc(v_spread, 1)

            def w_turn_probs(it):
                pe.wait_ge(probs_ready, it + 1)
                pe.wait_ge(v_masked, 4 * it + 3)
                for g in range(4):
                    last = pe.transpose(A0[:, g * 128:(g + 1) * 128],
                                        probs_n[:, g].rearrange("p h q -> p (h q)"), ident[:])
                last.then_inc(probs_turned, 1)

            def w_values(it):
                pe.wait_ge(probs_t_ready, it + 1)
                pe.wait_ge(v_masked, 4 * it + 4)
                for p in range(PAIRS):
                    wr, k = p // WPT, p % WPT
                    for odd in range(2):
                        col = (p // 4) * 128 + (p % 4) * 32 + odd * QUERIES
                        out = A1[64 * odd:64 * odd + 64, wr * HALF:(wr + 1) * HALF].rearrange(
                            "p (a c b) -> p a c b", a=WIN, b=WIN)[:, :, 2 * k + odd, :]
                        last = mm(out, v_heads[:, k, 2 * odd + wr, :], probs_t[:, col:col + QUERIES],
                                  start=True, stop=True)
                last.then_inc(av_done, 1)

            def w_project_out(it):
                pe.wait_ge(att_t_ready, 2 * it + 2)
                for c in range(CHUNKS):
                    last = mm(A0[0:CT, c * EMB:(c + 1) * EMB], att_t[:, c * CT:(c + 1) * CT], out_w[:],
                              start=True, stop=True)
                last.then_inc(h1_done, 1)

            def r_turn(src, bank, ready, count, done):
                pe.wait_ge(ready, count)
                for c in range(CHUNKS):
                    last = pe.transpose(bank[:, c * CT:(c + 1) * CT], src[:, c].rearrange("p a n -> p (a n)"),
                                        ident[0:CT, 0:CT])
                last.then_inc(done, 1)

            def r_project_qk(n):
                pe.wait_ge(xn_split_ready, n + 1)
                if later(n):
                    pe.wait_ge(gates_split_ready, n)
                for k, bank in ((0, B1), (1, B0)):
                    for s in range(2):
                        last = mm(bank[:, 0:BT], r_w[s][:, 2 * k:2 * k + 2].rearrange("p a b -> p (a b)"),
                                  xn_split[:], start=(s == 0), stop=(s == 1))
                last.then_inc(rqk_done, 1)

            def r_project_v(n):
                pe.wait_ge(rot_ready, n + 1)
                for c in range(CHUNKS):
                    for s in range(2):
                        last = mm(B1[0:CT, c * EMB:(c + 1) * EMB], xn_split[:, c * CT:(c + 1) * CT],
                                  r_w[s][:, 4], start=(s == 0), stop=(s == 1))
                last.then_inc(rv_done, 1)

            def r_scores(n):
                pe.wait_ge(rot_ready, n + 1)
                for c in range(CHUNKS):
                    cols = slice(c * CT, (c + 1) * CT)
                    last = mm(B0[0:CT, cols], k_t[:, cols], q_t[:, cols], start=True, stop=True)
                last.then_inc(kq_done, 1)
                for c in range(CHUNKS):
                    pe.transpose(B1[0:CT, 256 + c * EMB:256 + (c + 1) * EMB], k_t[:, c * CT:(c + 1) * CT],
                                        ident[0:EMB, 0:EMB])

            def r_state(n):
                pe.wait_ge(v2_ready, n + 1)
                pe.wait_ge(k_dec_ready, n + 1)
                pe.wait_ge(att_ready, n + 1)
                rows = CT if later(n) else 1
                for c in range(CHUNKS):
                    last = mm(B0[0:EMB, c * EMB:(c + 1) * EMB], k_dec[0:rows, c], v2[0:rows, c],
                              start=True, stop=True)
                last.then_inc(state_done, 1)

            def r_output(n):
                for c in range(CHUNKS):
                    mm(B1[0:CT, c * EMB:(c + 1) * EMB], att[:, c], v2[:, c], start=True, stop=True)
                pe.wait_ge(state_ready, n + 1)
                for c in range(CHUNKS):
                    last = mm(B1[0:CT, 256 + c * EMB:256 + (c + 1) * EMB], q_t[:, c * CT:(c + 1) * CT],
                              state[:, c], start=True, stop=True)
                last.then_inc(ret_done, 1)

            def r_gate(n, buf):
                pe.wait_ge(x2_split_ready, n + 1)
                for c in range(CHUNKS):
                    for s in range(2):
                        last = mm(B1[0:CT, c * EXPERTS:(c + 1) * EXPERTS], x2_split[buf][:, c * CT:(c + 1) * CT],
                                  gate_w[s][:], start=(s == 0), stop=(s == 1))
                last.then_inc(gl_done, 1)

            def r_turn_gates(n):
                pe.wait_ge(gates_ready, n + 1)
                for c in range(CHUNKS):
                    last = pe.transpose(B0[0:EXPERTS, c * CT:(c + 1) * CT], gates[:, c], ident[0:CT, 0:CT])
                last.then_inc(gates_turned, 1)

            def e_open(n, buf):
                if later(n):
                    pe.wait_ge(moe_added, n)
                for s in range(2):
                    mm(moe_ps[:, 0:BT], b2_w[s][:], gates_split[buf][:], start=(s == 0), stop=False,
                       skip_group_check=True)

            def e_up(n, e, buf):
                if later(n) or e >= 2:
                    pe.wait_ge(hidden_ready, EXPERTS * n + e - 1)
                for s in range(2):
                    last = mm(up_ps[e % 2][:, 0:BT], up_w[s][:, e], x2_split[buf][:], start=(s == 0), stop=(s == 1))
                last.then_inc(up_done, 1)

            def e_spread_gate(n, e, buf):
                if e == 0:
                    pe.wait_ge(gates_split_ready, n + 1)
                if later(n) or e:
                    pe.wait_ge(gated_ready, EXPERTS * n + e)
                mm(gate_ps[:, 0:BT], sel[:, e], gates_split[buf][:], start=True, stop=True).then_inc(gate_done, 1)

            def e_down(n, e):
                pe.wait_ge(gated_ready, EXPERTS * n + e + 1)
                half = 64 * (e % 2)
                mm(moe_ps[half:half + 64, 0:BT], down_w[:, e], gated[:, e % GATED_BUFS], start=False,
                   stop=(e >= EXPERTS - 2), skip_group_check=True).then_inc(down_done, 1)

            def e_fold(n):
                pe.wait_ge(moe_copied, n + 1)
                for c in range(CHUNKS):
                    last = mm(moe_ps[0:CT, c * EMB:(c + 1) * EMB], moe_sb[:, c * CT:(c + 1) * CT], fold[:],
                              start=True, stop=True)
                last.then_inc(moe_folded, 1)

            def slot(s, odd):
                for e in range(EXPERTS):
                    def at(step, blocks=ALL_BLOCKS + 1):
                        return due(s, odd, e, step, blocks)

                    for k in range(EXPERTS):
                        for n, buf in at(EXPERT_AT + k): e_up(n, k, buf)
                    for n, buf in at(PE_AT["open"]): e_open(n, buf)
                    for k in range(EXPERTS):
                        for n, buf in at(max(EXPERT_AT + k + DOWN_LAG, PE_AT["open"])): e_down(n, k)
                    for it, _ in at(PE_AT["qk"], ALL_BLOCKS): w_project_qk(it)
                    for it, _ in at(PE_AT["v"], ALL_BLOCKS): w_project_v(it)
                    for j in range(2):
                        for it, _ in at(PE_AT["spread"][j], ALL_BLOCKS): w_spread_v(it, j)
                    for it, _ in at(PE_AT["scores"], ALL_BLOCKS): w_scores(it)
                    for j in range(2, 4):
                        for it, _ in at(PE_AT["spread"][j], ALL_BLOCKS): w_spread_v(it, j)
                    for it, _ in at(PE_AT["probs"], ALL_BLOCKS): w_turn_probs(it)
                    for it, _ in at(PE_AT["values"], ALL_BLOCKS): w_values(it)
                    for it, _ in at(PE_AT["out"], ALL_BLOCKS): w_project_out(it)
                    for n, _ in at(PE_AT["xn"]):
                        if later(n):
                            pe.wait_ge(diff_ready, n)
                        r_turn(xn, B1, xn_ready, n + 1, xn_turned)
                    for n, _ in at(PE_AT["rqk"]): r_project_qk(n)
                    for n, _ in at(PE_AT["rscores"]): r_scores(n)
                    for n, _ in at(PE_AT["rv"]): r_project_v(n)
                    for n, _ in at(PE_AT["state"]): r_state(n)
                    for n, _ in at(PE_AT["output"]): r_output(n)
                    for n, buf in at(PE_AT["x2"]): r_turn(x2[buf], B0, x2_ready, n + 1, x2_turned)
                    for n, buf in at(PE_AT["logits"]): r_gate(n, buf)
                    for n, _ in at(PE_AT["gates"]): r_turn_gates(n)
                    for n, _ in at(PE_AT["fold"]): e_fold(n)
                    for k in range(EXPERTS):
                        for n, buf in at(EXPERT_AT + k): e_spread_gate(n, k, buf)

            pe.wait_ge(setup, N_SETUP)
            pe.wait_ge(loaded, N_LOADED)
            pe.wait_ge(filled, N_FILLED)
            for s in range(-1, LOOP_FROM):
                slot(s, s % 2)
            with pe.Fori(LOOP_FROM // 2, ALL_BLOCKS // 2) as pair:
                slot(2 * pair, 0)
                slot(2 * pair + 1, 1)
            for s in range(ALL_BLOCKS, ALL_BLOCKS + 3):
                slot(s, s % 2)

        @block.scalar
        def _(act):
            A = act.activation

            def w_split(it):
                act.wait_ge(x_loaded, 32 * it + 32)
                if later(it):
                    act.wait_ge(v_done, it)
                A(x_split[:], x_in[:], ACT.Copy).then_inc(x_high, 1)

            def w_evac_qk(it):
                act.wait_ge(qk_done, it + 1)
                A(k_sb[:], A0[:, HALF:BT], ACT.Identity, bias=qk_bias[:, 1:2]).then_inc(k_copied, 1)
                for odd in range(2):
                    rows = slice(64 * odd, 64 * odd + 64)
                    A(q_zero[rows, :, odd, :], A0[rows, 0:HALF].rearrange("p (w q) -> p w q", q=QUERIES),
                      ACT.Identity, bias=q_bias[rows, 0:1], scale=float(HD) ** -0.5).then_inc(q_ready, 1)

            def w_exp(it):
                act.wait_ge(shifted_ready, it + 1)
                A(probs[:], shifted[:], ACT.Exp).then_inc(exp_ready, 1)

            def w_evac_probs(it):
                act.wait_ge(probs_turned, it + 1)
                A(probs_t[:], A0[:], ACT.Copy).then_inc(probs_t_ready, 1)

            def w_evac_att(it):
                act.wait_ge(av_done, it + 1)
                for odd in range(2):
                    A(att_t[0:EMB, :].rearrange("p (a c b) -> p a c b", a=ROWS, b=WIN)[:, :, odd::2, :],
                      A1[64 * odd:64 * odd + 64, 0:BT].rearrange("p (a c b) -> p a c b", a=ROWS, b=WIN)[:, :, odd::2, :],
                      ACT.Copy).then_inc(att_t_ready, 1)

            def w_evac_h1(it, buf):
                act.wait_ge(h1_done, it + 1)
                A(h1[buf][:].rearrange("p c n -> p (c n)"), A0[0:CT, 0:256], ACT.Copy).then_inc(h1_ready, 1)

            def r_split(n):
                act.wait_ge(xn_turned, n + 1)
                A(xn_split[:], B1[:, 0:BT], ACT.Copy).then_inc(xn_high, 1)

            def r_evac_kv(n):
                variant = 0 if later(n) else 1
                act.wait_ge(rv_done, n + 1)
                A(k_dec[:].rearrange("p c n -> p (c n)"), B1[0:CT, 256:512], ACT.Copy,
                  scale=key_decay[:, variant:variant + 1]).then_inc(k_dec_ready, 1)
                A(v2[:].rearrange("p c n -> p (c n)"), B1[0:CT, 0:256], ACT.Copy).then_inc(v2_ready, 1)

            def r_split2(n, buf):
                act.wait_ge(x2_turned, n + 1)
                A(x2_split[buf][:], B0[:, 0:BT], ACT.Copy).then_inc(x2_high, 1)

            def r_gate_exp(n):
                act.wait_ge(diff_ready, n + 1)
                A(top_exp[:], top_diff[:], ACT.Exp).then_inc(gexp_ready, 1)

            def r_split_gates(n, buf):
                act.wait_ge(gates_turned, n + 1)
                A(gates_split[buf][0:EXPERTS, :], B0[0:EXPERTS, 0:BT], ACT.Copy).then_inc(gates_high, 1)

            def e_hidden(n, e):
                act.wait_ge(up_done, EXPERTS * n + e + 1)
                if later(n) or e >= HIDDEN_BUFS:
                    act.wait_ge(gated_ready, EXPERTS * n + e - HIDDEN_BUFS + 1)
                A(hidden[:, e % HIDDEN_BUFS], up_ps[e % 2][:, 0:BT], ACT.Relu, bias=up_bias[:, e:e + 1]).then_inc(hidden_ready, 1)

            def e_copy(n):
                act.wait_ge(down_done, EXPERTS * n + EXPERTS)
                A(moe_sb[:], moe_ps[:, 0:BT], ACT.Copy).then_inc(moe_copied, 1)

            def slot(s, odd):
                for e in range(EXPERTS):
                    def at(step, blocks=ALL_BLOCKS + 1):
                        return due(s, odd, e, step, blocks)

                    for it, _ in at(ACT_AT["x"], ALL_BLOCKS): w_split(it)
                    for k in range(EXPERTS):
                        for n, _ in at(EXPERT_AT + k): e_hidden(n, k)
                    for n, _ in at(ACT_AT["copy"]): e_copy(n)
                    for it, _ in at(ACT_AT["qk"], ALL_BLOCKS): w_evac_qk(it)
                    for it, _ in at(ACT_AT["exp"], ALL_BLOCKS): w_exp(it)
                    for it, _ in at(ACT_AT["probs"], ALL_BLOCKS): w_evac_probs(it)
                    for it, _ in at(ACT_AT["values"], ALL_BLOCKS): w_evac_att(it)
                    for it, buf in at(ACT_AT["out"], ALL_BLOCKS): w_evac_h1(it, 1 - buf)
                    for n, _ in at(ACT_AT["xn"]): r_split(n)
                    for n, _ in at(ACT_AT["kv"]): r_evac_kv(n)
                    for n, buf in at(ACT_AT["x2"]): r_split2(n, buf)
                    for n, _ in at(ACT_AT["exp_gate"]): r_gate_exp(n)
                    for n, buf in at(ACT_AT["gates"]): r_split_gates(n, buf)

            act.wait_ge(setup, N_SETUP)
            act.wait_ge(loaded, N_LOADED)
            act.wait_ge(filled, N_FILLED)
            for s in range(-1, LOOP_FROM):
                slot(s, s % 2)
            with act.Fori(LOOP_FROM // 2, ALL_BLOCKS // 2) as pair:
                slot(2 * pair, 0)
                slot(2 * pair + 1, 1)
            for s in range(ALL_BLOCKS, ALL_BLOCKS + 3):
                slot(s, s % 2)

        @block.vector
        def _(dve):
            TT, TS, CP = dve.tensor_tensor, dve.tensor_scalar, dve.tensor_copy

            made = [0]

            def did(ins):
                made[0] += 1
                ins.then_inc(setup, 1)

            def settle():
                dve.wait_ge(setup, made[0])

            dve.wait_ge(loaded, N_LOADED)
            dve.wait_ge(filled, N_FILLED)
            for odd in range(2):
                cols = slice(64 * odd, 64 * odd + 64)
                did(CP(q_even_odd[odd][0][:, cols], qk_raw[:, 0]))
                did(CP(k_even_odd[odd][0][:, cols], qk_raw[:, 1]))
            did(CP(v_w[0][:], v_raw[:]))
            did(CP(r_w[0][:], r_raw[:]))
            did(CP(gate_w[0][:], gate_raw[:]))
            did(CP(up_w[0][:], up_raw[:]))
            did(CP(b2_w[0][:], b2_raw[:]))
            settle()
            for odd in range(2):
                cols = slice(64 * odd, 64 * odd + 64)
                did(TT(q_even_odd[odd][1][:, cols], qk_raw[:, 0], q_even_odd[odd][0][:, cols].bitcast(F32), ALU.subtract))
                did(TT(k_even_odd[odd][1][:, cols], qk_raw[:, 1], k_even_odd[odd][0][:, cols].bitcast(F32), ALU.subtract))
            did(TT(v_w[1][:], v_raw[:], v_w[0][:].bitcast(F32), ALU.subtract))
            did(TT(r_w[1][:], r_raw[:], r_w[0][:].bitcast(F32), ALU.subtract))
            did(TT(gate_w[1][:], gate_raw[:], gate_w[0][:].bitcast(F32), ALU.subtract))
            did(TT(up_w[1][:], up_raw[:], up_w[0][:].bitcast(F32), ALU.subtract))
            did(TT(b2_w[1][:], b2_raw[:], b2_w[0][:].bitcast(F32), ALU.subtract))
            did(CP(sel[:], broadcast(sel_row[:], 2, 128)))
            wb = win_bias[:].rearrange("p a b q -> p (a b) q")
            did(TT(wb, wb, broadcast(pos_bias[:], 1, ALL_BLOCKS * 4), ALU.add))
            did(dve.memset(att_t[EMB:EMB + 1, :], 1.0))
            did(TS(q_bias[:], qk_bias[:, 0:1], float(HD) ** -0.5, None, ALU.mult))
            assert made[0] == N_SETUP
            settle()

            def w_split(it):
                dve.wait_ge(x_high, it + 1)
                TT(x_split[64:128, :], x_in[64:128, :], x_split[64:128, :].bitcast(F32), ALU.subtract).then_inc(x_ready, 1)

            def w_evac_v(it):
                dve.wait_ge(v_done, it + 1)
                TT(v_tok[:], A1[0:CT, 0:256].rearrange("p (t n) -> p t n", n=EMB), broadcast(v_bias[:], 1, 4),
                   ALU.add).then_inc(v_ready, 1)

            def w_softmax(it):
                ch = link(dve, chain1, it, 2)
                dve.wait_ge(s_done, it + 1)
                bias = win_bias[:, bass.ds(it, 1)].rearrange("p o g q -> p (o g) q")
                ch(TT(logits[:], A1[:].rearrange("p (g h q) -> p g h q", g=4, h=HEADS), broadcast(bias, 2, HEADS), ALU.add))
                ch(dve.tensor_reduce(row_max[:], logits[:], AX.X, ALU.max))
                TT(shifted[:], logits[:], broadcast(row_max[:], 3, QUERIES), ALU.subtract).then_inc(shifted_ready, 1)

            def w_normalise(it):
                ch = link(dve, chain_sums, it, 2)
                dve.wait_ge(exp_ready, it + 1)
                ch(dve.tensor_reduce(row_sum[:], probs[:], AX.X, ALU.add))
                ch(dve.reciprocal(row_inv[:], row_sum[:]))
                TT(probs_n[:], probs[:], broadcast(row_inv[:], 3, QUERIES), ALU.mult).then_inc(probs_ready, 1)

            def w_mask_v(it, j):
                dve.wait_ge(v_spread, 4 * it + j + 1)
                bank = (A0, A1)[j % 2]
                m = min(2, WPT - 2 * j)
                TT(v_heads[:, 2 * j:2 * j + m].rearrange("p k t n -> p (k t) n"),
                   bank[:, 0:256 * m].rearrange("p (a n) -> p a n", n=EMB),
                   broadcast(head_columns[:], 1, 4 * m), ALU.mult).then_inc(v_masked, 1)

            def norm_stats(src, k, n):
                ch = link(dve, chain_stats[k], n, 3)
                st, mv = stats[k], mean_var[k]
                for c in range(CHUNKS):
                    ins = dve.bn_stats(st[:, c], src[:, c])
                ch(ins)
                TT(mv[:, :, 0], st[:, :, 1], st[:, :, 4], ALU.add)
                TT(mv[:, :, 1], st[:, :, 1], st[:, :, 4], ALU.subtract)
                ch(TT(mv[:, :, 2], st[:, :, 2], st[:, :, 5], ALU.add))
                ch(dve.scalar_tensor_tensor(mv[:, :, 3], mv[:, :, 1], 0.25, mv[:, :, 1], ALU.mult, ALU.mult))
                dve.scalar_tensor_tensor(mv[:, :, 4], mv[:, :, 2], 1.0 / EMB, mv[:, :, 3],
                                         ALU.mult, ALU.add).then_inc(var_ready[k], 1)

            def norm_apply(src, k, dst, n, done):
                ch = link(dve, chain_apply[k], n, 1)
                ch(dve.scalar_tensor_tensor(centred[k][:], mean_var[k][:, :, 0:1].broadcast_to([CT, CHUNKS, EMB]), -0.5,
                                            src[:], ALU.mult, ALU.add))
                dve.wait_ge(rstd_ready[k], n + 1)
                if len(dst.shape) == 4:
                    ins = TT(dst[:], broadcast(centred[k][:], 2, 2), broadcast(broadcast(rstd[k][:], 2, 2), 3, EMB),
                             ALU.mult)
                else:
                    ins = TT(dst[:], centred[k][:], broadcast(rstd[k][:], 2, EMB), ALU.mult)
                ins.then_inc(done, 1)

            def r_norm1_stats(n, buf):
                if later(n):
                    dve.wait_ge(h1_ready, n)
                norm_stats(h1[buf], 0, n)

            def r_norm1(n, buf):
                norm_apply(h1[buf], 0, xn, n, xn_ready)

            def r_split(n):
                dve.wait_ge(xn_high, n + 1)
                TT(xn_split[64:128, :], B1[64:128, 0:BT], xn_split[64:128, :].bitcast(F32),
                   ALU.subtract).then_inc(xn_split_ready, 1)

            def r_rotate(n):
                if later(n):
                    position = ((n - 1) % BLOCKS) * BT + 1
                    cos, sin = cos_t[:, bass.ds(position, BT)], sin_t[:, bass.ds(position, BT)]
                else:
                    cos, sin = cls_cos[:], cls_sin[:]
                ch = link(dve, chain_rotate, n, 1)
                dve.wait_ge(rqk_done, n + 1)
                TT(rot_cos[:], B1[:, 0:BT], cos, ALU.mult)
                ch(TT(rot_sin[:], B0[:, 0:BT], sin, ALU.mult))
                TT(q_t[:], rot_cos[0:64, :], rot_sin[0:64, :], ALU.add)
                TT(k_t[:], rot_cos[64:128, :], rot_sin[64:128, :], ALU.add).then_inc(rot_ready, 1)

            def r_decay(n):
                variant = 0 if later(n) else 1
                dve.wait_ge(kq_done, n + 1)
                TT(att[:], B0[0:CT, 0:BT].rearrange("p (c n) -> p c n", n=CT),
                   broadcast(decay[:, variant], 1, CHUNKS), ALU.mult).then_inc(att_ready, 1)

            def r_state(n):
                if not later(n):
                    dve.wait_ge(state_done, 1)
                    CP(state_cls[:], B0[0:EMB, 0:EMB]).then_inc(state_ready, 1)
                    return
                ch = link(dve, chain_s, n - 1, 5)
                ch(TS(state_mid[:], state[:, CHUNKS], carry[:, 0, bass.ds(n, 1)], None, ALU.mult))
                ch(dve.scalar_tensor_tensor(state[:, 0], state_cls[:], carry[:, 1, bass.ds(n, 1)], state_mid[:],
                                            ALU.mult, ALU.add))
                dve.wait_ge(state_done, n + 1)
                for c in range(CHUNKS):
                    ins = dve.scalar_tensor_tensor(state[:, c + 1], state[:, c], GAMMA ** CT,
                                                   B0[0:EMB, c * EMB:(c + 1) * EMB], ALU.mult, ALU.add)
                    if c < CHUNKS - 1:
                        ch(ins)
                ins.then_inc(state_ready, 1)

            def r_residual(n, buf):
                ch = link(dve, chain_residual, n, 1)
                dve.wait_ge(ret_done, n + 1)
                ch(TT(h1_intra[:].rearrange("p c n -> p (c n)"), B1[0:CT, 0:256],
                      h1[buf][:].rearrange("p c n -> p (c n)"), ALU.add))
                if not isinstance(n, int) or n >= 2:
                    dve.wait_ge(h3_ready, n - 1)
                dve.scalar_tensor_tensor(h2[buf][:].rearrange("p c n -> p (c n)"), B1[0:CT, 256:512], query_decay[:, 0:1],
                                         h1_intra[:].rearrange("p c n -> p (c n)"), ALU.mult, ALU.add).then_inc(h2_ready, 1)

            def r_norm2_stats(n, buf):
                dve.wait_ge(h2_ready, n + 1)
                norm_stats(h2[buf], 1, n)

            def r_norm2(n, buf):
                norm_apply(h2[buf], 1, x2[buf], n, x2_ready)

            def r_split2(n, buf):
                dve.wait_ge(x2_high, n + 1)
                TT(x2_split[buf][64:128, :], B0[64:128, 0:BT], x2_split[buf][64:128, :].bitcast(F32),
                   ALU.subtract).then_inc(x2_split_ready, 1)

            def r_top(n):
                ch = link(dve, chain_top, n, 5)
                dve.wait_ge(gl_done, n + 1)
                ch(TT(gate_logits[:], B1[0:CT, 0:CHUNKS * EXPERTS].rearrange("p (c e) -> p c e", e=EXPERTS),
                      broadcast(gate_bias[:], 1, CHUNKS), ALU.add))
                dve.tensor_reduce(top_sum[:], gate_logits[:], AX.X, ALU.max)
                for c in range(CHUNKS):
                    ins = dve.max(top_val[:, c], gate_logits[:, c])
                ch(ins)
                TT(top_diff[:], top_val[:, :, 1], top_val[:, :, 0], ALU.subtract).then_inc(diff_ready, 1)
                for c in range(CHUNKS):
                    ins = dve.max_index(top_idx[:, c], top_val[:, c], gate_logits[:, c])
                ch(ins)
                ch(CP(top_id[:], top_idx[:, :, 0:2]))
                for k in range(TOP):
                    ins = TT(one_hot[:, k], broadcast(expert_ids[:], 1, CHUNKS),
                             top_id[:, :, k:k + 1].broadcast_to([CT, CHUNKS, EXPERTS]), ALU.is_equal)
                ch(ins)

            def r_gates(n):
                ch = link(dve, chain_gates, n, 4)
                dve.wait_ge(gexp_ready, n + 1)
                ch(TS(top_den[:], top_exp[:], 1.0, None, ALU.add))
                ch(dve.reciprocal(top_w[:, 0], top_den[:]))
                ch(TT(top_w[:, 1], top_w[:, 0], top_exp[:], ALU.mult))
                for k in range(TOP):
                    ins = TT(gates_a[:, k], one_hot[:, k], broadcast(top_w[:, k], 2, EXPERTS), ALU.mult)
                ch(ins)
                TT(gates[:], gates_a[:, 0], gates_a[:, 1], ALU.add).then_inc(gates_ready, 1)

            def r_split_gates(n, buf):
                dve.wait_ge(gates_high, n + 1)
                TT(gates_split[buf][32:32 + EXPERTS, :], B0[0:EXPERTS, 0:BT], gates_split[buf][0:EXPERTS, :].bitcast(F32),
                   ALU.subtract).then_inc(gates_split_ready, 1)

            def e_gate(n, e):
                dve.wait_ge(hidden_ready, EXPERTS * n + e + 1)
                if later(n) or e >= GATED_BUFS:
                    dve.wait_ge(down_done, EXPERTS * n + e - GATED_BUFS + 1)
                dve.wait_ge(gate_done, EXPERTS * n + e + 1)
                TT(gated[:, e % GATED_BUFS], gate_ps[:, 0:BT], hidden[:, e % HIDDEN_BUFS], ALU.mult).then_inc(gated_ready, 1)

            def e_residual(n, buf):
                dve.wait_ge(moe_folded, n + 1)
                TT(res[:].rearrange("p c n -> p (c n)"), moe_ps[0:CT, 0:256].rearrange("p (c n) -> p c n", n=EMB),
                   x2[buf][:, :, 0], ALU.add).then_inc(moe_added, 1)
                dve.wait_ge(moe_added, n + 1)
                norm_stats(res, 2, n)

            def slot(s, odd):
                for e in range(EXPERTS):
                    def at(step, blocks=ALL_BLOCKS + 1):
                        return due(s, odd, e, step, blocks)

                    for it, _ in at(DVE_AT["x"], ALL_BLOCKS): w_split(it)
                    for k in range(EXPERTS):
                        for n, _ in at(EXPERT_AT + k): e_gate(n, k)
                    for n, buf in at(DVE_AT["added"]): e_residual(n, buf)
                    for n, _ in at(DVE_AT["norm3"]): norm_apply(res, 2, normed3, n, normed3_ready)
                    for it, _ in at(DVE_AT["v"], ALL_BLOCKS): w_evac_v(it)
                    for j in range(2):
                        for it, _ in at(DVE_AT["mask"][j], ALL_BLOCKS): w_mask_v(it, j)
                    for it, _ in at(DVE_AT["softmax"], ALL_BLOCKS): w_softmax(it)
                    for it, _ in at(DVE_AT["normalise"], ALL_BLOCKS): w_normalise(it)
                    for j in range(2, 4):
                        for it, _ in at(DVE_AT["mask"][j], ALL_BLOCKS): w_mask_v(it, j)
                    for n, buf in at(DVE_AT["xn"]): r_split(n)
                    for n, _ in at(DVE_AT["rotate"]): r_rotate(n)
                    for n, _ in at(DVE_AT["decay"]): r_decay(n)
                    for n, _ in at(DVE_AT["state"]): r_state(n)
                    for n, buf in at(DVE_AT["residual"]): r_residual(n, buf)
                    for n, buf in at(DVE_AT["stats2"]): r_norm2_stats(n, buf)
                    for n, buf in at(DVE_AT["norm2"]): r_norm2(n, buf)
                    for n, buf in at(DVE_AT["x2"]): r_split2(n, buf)
                    for n, _ in at(DVE_AT["top"]): r_top(n)
                    for n, _ in at(DVE_AT["gates"]): r_gates(n)
                    for n, buf in at(DVE_AT["gates_low"]): r_split_gates(n, buf)
                    for n, buf in at(DVE_AT["stats1"]): r_norm1_stats(n, buf)
                    for n, buf in at(DVE_AT["norm1"]): r_norm1(n, buf)

            for s in range(-1, LOOP_FROM):
                slot(s, s % 2)
            with dve.Fori(LOOP_FROM // 2, ALL_BLOCKS // 2) as pair:
                slot(2 * pair, 0)
                slot(2 * pair + 1, 1)
            for s in range(ALL_BLOCKS, ALL_BLOCKS + 3):
                slot(s, s % 2)

        @block.gpsimd
        def _(pool):
            TT = pool.tensor_tensor

            cleared = [q_even_odd[0][0], q_even_odd[0][1], q_even_odd[1][0], q_even_odd[1][1],
                       k_even_odd[0][0], k_even_odd[0][1], k_even_odd[1][0], k_even_odd[1][1]]
            for t in cleared:
                pool.memset(t[:].bitcast(F32), 0.0)
            pool.memset(b2_raw[:], 0.0)
            for t in gates_split:
                pool.memset(t[:].bitcast(F32), 0.0)
            pool.memset(q_zero[:], 0.0).then_inc(filled, 1)
            pool.memset(state[:], 0.0).then_inc(filled, 1)
            pool.memset(cls_cos[:], 1.0).then_inc(filled, 1)
            pool.memset(cls_sin[:], 0.0).then_inc(filled, 1)
            pool.memset(eps_t[:], EPS)
            pool.memset(power[:], -0.5).then_inc(filled, 1)
            pool.memset(h3[:], 0.0).then_inc(stored, 16)

            def w_expand_k(it):
                pool.wait_ge(k_copied, it + 1)
                pool.tensor_tensor(
                    k_heads[:], broadcast(k_sb[:].rearrange("p (w q) -> p w q", q=QUERIES), 2, HEADS),
                    broadcast(broadcast(head_of_channel[:], 1, PAIRS), 3, QUERIES), ALU.mult).then_inc(k_ready, 1)

            def inverse_root(n, k):
                ch = link(pool, pool_chain[k], n, 1)
                pool.wait_ge(var_ready[k], n + 1)
                ch(TT(var_eps[k][:], mean_var[k][:, :, 4], eps_t[:], ALU.add))
                TT(rstd[k][:], var_eps[k][:], power[:], ALU.pow).then_inc(rstd_ready[k], 1)

            def e_finish(n, buf):
                ch = link(pool, pool_finish, n, 2)
                pool.wait_ge(normed3_ready, n + 1)
                pool.wait_ge(stored, 16 * n + 16)
                ch(TT(h3[:], normed3[:], broadcast(ln_gamma[:], 1, CHUNKS), ALU.mult))
                ch(TT(h3[:], h3[:], broadcast(ln_beta[:], 1, CHUNKS), ALU.add))
                TT(h3[:], h3[:], h2[buf][:], ALU.add).then_inc(h3_ready, 1)

            def slot(s, odd):
                for e in range(EXPERTS):
                    def at(step, blocks=ALL_BLOCKS + 1):
                        return due(s, odd, e, step, blocks)

                    for n, _ in at(POOL_AT["root1"]): inverse_root(n, 0)
                    for n, _ in at(POOL_AT["root2"]): inverse_root(n, 1)
                    for n, _ in at(POOL_AT["root3"]): inverse_root(n, 2)
                    for it, _ in at(POOL_AT["keys"], ALL_BLOCKS): w_expand_k(it)
                    for n, buf in at(POOL_AT["finish"]): e_finish(n, buf)

            pool.wait_ge(loaded, N_LOADED)
            pool.wait_ge(filled, N_FILLED)
            for s in range(-1, LOOP_FROM):
                slot(s, s % 2)
            with pool.Fori(LOOP_FROM // 2, ALL_BLOCKS // 2) as pair:
                slot(2 * pair, 0)
                slot(2 * pair + 1, 1)
            for s in range(ALL_BLOCKS, ALL_BLOCKS + 3):
                slot(s, s % 2)


def constants():
    t = {}
    p = np.arange(128)
    f = np.float32
    rows = np.zeros((QUERIES, QUERIES))
    s = WIN * (WIN // 2)
    rows[-s:, :-s] = MASKED
    rows[:-s, -s:] = MASKED
    cols = rows.reshape(WIN, WIN, WIN, WIN).transpose(1, 0, 3, 2).reshape(QUERIES, QUERIES)
    mask = np.zeros((4, 2, QUERIES, IMAGES, BLOCKS, 4, QUERIES), f)
    for pair in range(PAIRS):
        g, c = divmod(pair, 4)
        wr, k = divmod(pair, WPT)
        if wr == 1:
            mask[c, :, :, :, BLOCKS - 1, g, :] += rows[:, None, :]
        if k == WPT - 1:
            mask[c, 1, :, :, :, g, :] += cols[:, None, None, :]
    t["win_mask"] = mask.reshape(128, -1)
    t["head_of_channel"] = ((p[:, None] % EMB) // HD == np.arange(HEADS)).astype(f)
    t["head_columns"] = (p[:, None] // QUERIES == np.arange(EMB) // HD).astype(f)
    q = np.arange(CT)
    t["pick"] = ((q[:, None, None] // QUERIES == np.arange(WPT)[:, None]) &
                 (q[:, None, None] % QUERIES == p % QUERIES)).astype(f).reshape(CT, -1)
    t["ident"] = np.eye(128, dtype=f)
    inv = f(1.0) / np.power(f(THETA), np.arange(0, EMB, 2, dtype=f) / f(EMB), dtype=f)
    angle = np.arange(SEQ, dtype=f)[:, None] * inv[None, :]
    cos, sin = np.cos(angle).astype(f), np.sin(angle).astype(f)
    t["cos"] = np.tile(np.repeat(cos, 2, axis=1).T, (2, 1)).astype(f)
    t["sin"] = np.tile(np.stack([-sin, sin], axis=2).reshape(SEQ, EMB).T, (2, 1)).astype(f)
    n = np.arange(CT)
    diff = n[None, :] - n[:, None]
    within = np.where(diff >= 0, GAMMA ** np.maximum(diff, 0).astype(np.float64), 0.0)
    t["decay"] = np.stack([within, np.eye(CT)], axis=1).astype(f).reshape(CT, -1)
    t["key_decay"] = np.stack([GAMMA ** (CT - 1.0 - n), np.ones(CT)], axis=1).astype(f)
    t["query_decay"] = (GAMMA ** (n + 1.0))[:, None].astype(f)
    first = (np.arange(ALL_BLOCKS + 1) - 1) % BLOCKS == 0
    t["carry"] = np.tile(np.concatenate([~first, first]).astype(f), (EMB, 1))
    t["expert_ids"] = np.tile(np.arange(EXPERTS, dtype=f), (CT, 1))
    e = np.arange(EXPERTS)
    t["sel_row"] = ((p[:, None] == e) | (p[:, None] == 32 + e)).astype(f)
    t["fold"] = np.tile(np.eye(EMB, dtype=f), (2, 1))
    return {k: np.ascontiguousarray(v) for k, v in t.items()}


def lay_out(d):
    a = {}
    x = np.roll(d["x"], (-(WIN // 2), -(WIN // 2)), axis=(2, 3))
    x = x.reshape(IMAGES, EMB, BLOCKS, 2, WIN, WPT, 2, WIN)
    a["x"] = x.transpose(0, 2, 1, 6, 3, 5, 4, 7).reshape(ALL_BLOCKS, EMB, BT)
    w1 = d["L0_tok_w1"].reshape(HD, HEADS, 3, EMB).transpose(2, 3, 1, 0).reshape(3, EMB, EMB)
    b1 = d["L0_tok_b1"].reshape(HD, HEADS, 3).transpose(2, 1, 0).reshape(3, EMB)
    a["w_qk"] = w1[0:2].transpose(1, 0, 2)
    a["w_v"] = w1[2]
    a["b_qk"] = b1[0:2].T
    a["b_v"] = np.tile(b1[2], (CT, 1))
    a["w_out"] = np.concatenate([d["L0_tok_w2"].T, d["L0_tok_b2"][None]], axis=0)
    c = np.array([[i, j] for i in range(WIN) for j in range(WIN)])
    rel = c[None, :, :] - c[:, None, :] + WIN - 1
    a["pos"] = np.tile(d["L0_tok_pos_emb"][rel[..., 0], rel[..., 1]], (128 // QUERIES, 1))
    swap = np.arange(EMB) ^ 1
    wq, wk = d["L0_attn_W_Q"], d["L0_attn_W_K"]
    a["w_ret"] = np.stack([wq, wk, wq[:, swap], wk[:, swap], d["L0_attn_W_V"]], axis=1)
    a["w_gate"] = d["L0_ffn_gate_w"]
    a["b_gate"] = np.tile(d["L0_ffn_gate_b"], (CT, 1))
    a["w_up"] = d["L0_ffn_w1"].transpose(1, 0, 2)
    a["b_up"] = d["L0_ffn_b1"].T
    a["w_down"] = d["L0_ffn_w2"].transpose(1, 0, 2)
    a["b_down"] = d["L0_ffn_b2"]
    a["gamma"] = np.tile(d["L0_ffn_gamma"], (CT, 1))
    a["beta"] = np.tile(d["L0_ffn_beta"], (CT, 1))
    a["cls"] = np.tile(d["cls_tok"].reshape(1, EMB), (CT, CHUNKS))
    return {k: np.ascontiguousarray(v) for k, v in a.items()}


def kernel(**inputs):
    import concourse.bacc as bacc
    from concourse.bass_utils import run_bass_kernel_spmd

    arrays = lay_out({k: np.asarray(v) for k, v in inputs.items()})
    arrays.update(constants())
    nc = bacc.Bacc("TRN2", target_bir_lowering=False, num_devices=1)
    aps = {k: nc.dram_tensor("in_" + k, v.shape, mybir.dt.from_np(v.dtype), kind="ExternalInput").ap()
           for k, v in arrays.items()}
    out = nc.dram_tensor("out_y", ((ALL_BLOCKS + 1) * CHUNKS, CT, EMB), F32, kind="ExternalOutput").ap()
    build_tower(nc, aps, out)
    r = run_bass_kernel_spmd(nc, [{"in_" + k: v for k, v in arrays.items()}], core_ids=[0])
    got = np.asarray(r.results[0]["out_y"])
    cls = np.tile(got[0, 0].reshape(1, 1, EMB), (IMAGES, 1, 1))
    return np.concatenate([cls, got[CHUNKS:].reshape(IMAGES, SIDE * SIDE, EMB)], axis=1)
```

```python
from contextlib import ExitStack

import numpy as np

import concourse.bass as bass
from concourse import mybir

F32 = mybir.dt.float32
F32R = mybir.dt.float32r
U32 = mybir.dt.uint32
ALU = mybir.AluOpType
ACT = mybir.ActivationFunctionType
AX = mybir.AxisListType

IMAGES, EMB, SIDE = 4, 64, 56
HEADS, WIN, HD = 8, 4, 8
EXPERTS, FF, TOP = 16, 128, 2
GAMMA, THETA, EPS = 0.96875, 10000.0, 1e-5
QUERIES = WIN * WIN
ROWS = 2 * WIN
BT = ROWS * SIDE
BLOCKS = SIDE // ROWS
ALL_BLOCKS = IMAGES * BLOCKS
CT = 2 * SIDE
CHUNKS = BT // CT
PAIRS = BT // QUERIES // 2
WPT = CT // QUERIES
HALF = BT // 2
SEQ = 1 + SIDE * SIDE
MASKED = -1e30
HIDDEN_BUFS, GATE_BUFS, PRODUCT_BUFS = 8, 8, 4
COUPLES = EXPERTS // 2

LOOP_FROM = 2

PE_AT = dict(qk=-2, v=-2, spread=(2, 2, 6, 10), scores=6, probs=11, values=12, out=13, xn=1, rqk=2, rscores=6, rv=6,
             state=7, output=8, x2=12, logits=13, gates=16, open=17, fold=37)
ACT_AT = dict(rotate=4, x=-13, qk=-1, v=-1, exp=7, probs=10, values=12, out=13, xn=1, kv=6, x2=12, exp_gate=14,
              gates=16, open=17)
DVE_AT = dict(v=0, mask=(2, 2, 9, 10), softmax=5, normalise=8, stats1=-4, norm1=-1, rotate=3, decay=5, state=7,
              residual=9, stats2=9, norm2=10, top=13, gates=14, added=36)
POOL_AT = dict(x=-11, keys=3, shift=6, normalise=8, rotate=4, root1=-6, root2=8, root3=38, finish=38)
SETUP_STEP = 6
EXPERT_AT = 17
GATE_AT = EXPERT_AT + 1
DOWN_LAG = 3
PRODUCT_AT = EXPERT_AT + 3
ADD_AT = EXPERT_AT + 4

PACKED = {
    "window": (("w_qk", 128, (2, EMB)), ("w_v", 128, (EMB,)), ("b_qk", 128, (2,)), ("b_v", 128, (1,)),
               ("w_out", EMB + 1, (EMB,)), ("win_mask", 128, (BLOCKS, 4, QUERIES)), ("pos", 128, (QUERIES,)),
               ("head_of_channel", 128, (HEADS,)), ("head_columns", 128, (EMB,)), ("pick", CT, (WPT, 128)),
               ("ident", 128, (128,))),
    "retention": (("w_ret", 128, (5, EMB)), ("decay", CT, (2, CT)), ("key_decay", CT, (2,)), ("query_decay", CT, (1,)),
                  ("w_gate", 128, (EXPERTS,)), ("b_gate", CT, (EXPERTS,)), ("expert_ids", CT, (EXPERTS,)),
                  ("carry", EMB, (2, ALL_BLOCKS + 1))),
    "rotary": (("cos", 128, (1 + SIDE * SIDE,)), ("sin", 128, (1 + SIDE * SIDE,))),
    "experts": (("w_up", 128, (EXPERTS, FF)), ("b_up", FF, (EXPERTS,)), ("w_down", FF, (EXPERTS, EMB)),
                ("b_down", 128, (128,)), ("sel_row", 128, (EXPERTS,)), ("fold", 128, (EMB,)),
                ("gamma", CT, (EMB,)), ("beta", CT, (EMB,))),
}


def later(n):
    return not isinstance(n, int) or n > 0


def broadcast(ap, axis, n):
    ap = ap.unsqueeze(axis)
    shape = list(ap.shape)
    shape[axis] = n
    return ap.broadcast_to(shape)


def build_tower(nc, I, y):
    ctx = ExitStack()
    with ctx:
        def sb(name, shape, dt=F32):
            return ctx.enter_context(nc.sbuf_tensor(name, shape, dt))

        def ps(name, shape):
            return ctx.enter_context(nc.psum_tensor(name, shape, F32))

        def sem(name):
            return ctx.enter_context(nc.semaphore(name))

        packed, views = {}, {}
        for group, parts in PACKED.items():
            widths = [int(np.prod(dims)) for _, _, dims in parts]
            packed[group] = sb(f"packed_{group}", [128, sum(widths)])
            for (name, rows, dims), width, end in zip(parts, widths, np.cumsum(widths)):
                view = packed[group][0:rows, int(end) - width:int(end)]
                letters = "abc"[:len(dims)]
                views[name] = view if len(dims) == 1 else view.rearrange(
                    f"p ({' '.join(letters)}) -> p {' '.join(letters)}", **dict(zip(letters, dims)))
        qk_raw = views["w_qk"]
        q_even_odd = [[sb(f"q_w{p}{s}", [128, 128], F32R) for s in "hl"] for p in "eo"]
        k_even_odd = [[sb(f"k_w{p}{s}", [128, 128], F32R) for s in "hl"] for p in "eo"]
        v_raw = views["w_v"]
        v_w = [sb(f"v_w{s}", [128, EMB], F32R) for s in "hl"]
        qk_bias = views["b_qk"]
        q_bias = sb("q_bias", [128, 1])
        v_bias = views["b_v"]
        out_w = views["w_out"]
        win_bias = views["win_mask"]
        pos_bias = views["pos"]
        head_of_channel = views["head_of_channel"]
        head_columns = views["head_columns"]
        pick_raw = views["pick"]
        pick = sb("pick", [CT, WPT, 128], F32R)
        ident = views["ident"]
        r_raw = views["w_ret"]
        r_w = [sb(f"r_w{s}", [128, 5, EMB], F32R) for s in "hl"]
        cos_t = views["cos"]
        sin_t = views["sin"]
        cls_cos = sb("cls_cos", [128, BT])
        cls_sin = sb("cls_sin", [128, BT])
        decay = views["decay"]
        key_decay = views["key_decay"]
        query_decay = views["query_decay"]
        gate_raw = views["w_gate"]
        gate_w = [sb(f"gate_w{s}", [128, EXPERTS], F32R) for s in "hl"]
        gate_bias = views["b_gate"]
        expert_ids = views["expert_ids"]
        up_raw = views["w_up"]
        up_w = [sb(f"up_w{s}", [128, EXPERTS, FF], F32R) for s in "hl"]
        up_bias = views["b_up"]
        down_w = views["w_down"]
        b2_raw = views["b_down"]
        b2_w = [sb(f"b2_w{s}", [128, 128], F32R) for s in "hl"]
        sel_row = views["sel_row"]
        sel = sb("sel", [128, EXPERTS, EMB], F32R)
        fold = views["fold"]
        ln_gamma = views["gamma"]
        ln_beta = views["beta"]
        power = sb("power", [CT, CHUNKS])
        eps_t = sb("eps_t", [CT, CHUNKS])

        x_in = sb("x_in", [128, BT])
        x_split = sb("x_split", [128, BT], F32R)
        k_sb = sb("k_sb", [128, HALF])
        q_zero = sb("q_zero", [128, PAIRS, 2, QUERIES])
        k_heads = sb("k_heads", [128, PAIRS, HEADS, QUERIES])
        v_parts = [sb(f"v_part{s}", [CT, 4 * EMB], F32R) for s in "hl"]
        v_heads = sb("v_heads", [128, WPT, 4, EMB])
        logits = sb("logits", [128, 4, HEADS, QUERIES])
        shifted = sb("shifted", [128, 4, HEADS, QUERIES])
        probs = sb("probs", [128, 4, HEADS, QUERIES])
        probs_n = sb("probs_n", [128, 4, HEADS, QUERIES])
        row_max = sb("row_max", [128, 4, HEADS])
        row_sum = sb("row_sum", [128, 4, HEADS])
        row_inv = sb("row_inv", [128, 4, HEADS])
        probs_t = sb("probs_t", [128, BT + 64])
        att_t = sb("att_t", [EMB + 1, BT])
        h1 = [sb(f"h1_{i}", [CT, CHUNKS, EMB]) for i in range(2)]
        xn_full = sb("xn_full", [CT, CHUNKS, EMB])
        xn = sb("xn", [CT, CHUNKS, 2, EMB], F32R)
        stats, mean_var, var_eps, rstd = (
            [sb(f"{name}{k}", shape) for k in range(3)]
            for name, shape in (("stats", [CT, CHUNKS, 6]), ("mean_var", [CT, CHUNKS, 2]), ("var_eps", [CT, CHUNKS]),
                                ("rstd", [CT, CHUNKS])))
        spare = sb("spare", [1, 1])
        xn_split = sb("xn_split", [128, BT], F32R)
        rot_cos = sb("rot_cos", [128, BT])
        rot_sin = sb("rot_sin", [128, BT])
        qk_rot = sb("qk_rot", [128, BT])
        k_t = sb("k_t", [EMB, BT])
        v2 = sb("v2", [CT, CHUNKS, EMB])
        att = sb("att", [CT, CHUNKS, CT])
        k_dec = sb("k_dec", [CT, CHUNKS, EMB])
        state = sb("state", [EMB, CHUNKS + 1, EMB])
        state_cls = sb("state_cls", [EMB, EMB])
        state_mid = sb("state_mid", [EMB, EMB])
        carry = views["carry"]
        h1_intra = sb("h1_intra", [CT, CHUNKS, EMB])
        h2 = [sb(f"h2_{i}", [CT, CHUNKS, EMB]) for i in range(2)]
        x2 = [sb(f"x2_{i}", [CT, CHUNKS, EMB]) for i in range(2)]
        x2_parts = sb("x2_parts", [CT, CHUNKS, 2, EMB], F32R)
        gate_logits = sb("gate_logits", [CT, CHUNKS, EXPERTS])
        top_val = sb("top_val", [CT, CHUNKS, 8])
        top_idx = sb("top_idx", [CT, CHUNKS, 8], U32)
        top_id = sb("top_id", [CT, CHUNKS, 2])
        top_diff = sb("top_diff", [CT, CHUNKS])
        top_exp = sb("top_exp", [CT, CHUNKS])
        top_den = sb("top_den", [CT, CHUNKS])
        top_w = sb("top_w", [CT, 2, CHUNKS])
        one_hot = sb("one_hot", [CT, 2, CHUNKS, EXPERTS])
        gates_a = sb("gates_a", [CT, 2, CHUNKS, EXPERTS])
        gates = sb("gates", [CT, CHUNKS, EXPERTS])
        gates_parts = sb("gates_parts", [CT, CHUNKS, 2, EXPERTS], F32R)
        x2_split = [sb(f"x2_split{i}", [128, BT], F32R) for i in range(2)]
        gates_split = [sb(f"gates_split{i}", [128, BT], F32R) for i in range(2)]
        hidden = sb("hidden", [128, HIDDEN_BUFS, BT])
        gate_rows = sb("gate_rows", [128, GATE_BUFS, BT])
        products = sb("products", [128, PRODUCT_BUFS, BT])
        total = [sb(f"total{i}", [128, BT]) for i in range(2)]
        res = sb("res", [CT, CHUNKS, EMB])
        centred3 = sb("centred3", [CT, CHUNKS, EMB])
        normed3 = sb("normed3", [CT, CHUNKS, EMB])
        h3 = sb("h3", [CT, CHUNKS, EMB])

        A0, A1 = (ps(f"win{i}", [128, 512]) for i in range(2))
        B0, B1 = (ps(f"ret{i}", [128, 512]) for i in range(2))
        up_ps = [ps(f"up{i}", [128, 512]) for i in range(2)]
        gate_ps = ps("gate", [128, 512])
        down_ps = ps("down", [128, 512])

        loaded = {group: sem(f"loaded_{group}") for group in PACKED}
        filled = sem("filled")
        setup = sem("setup")
        x_loaded = sem("x_loaded")
        x_high = sem("x_high")
        x_ready = sem("x_ready")
        qk_done = sem("qk_done")
        v_done = sem("v_done")
        q_ready = sem("q_ready")
        k_copied = sem("k_copied")
        k_ready = sem("k_ready")
        v_high = sem("v_high")
        v_ready = sem("v_ready")
        s_done = sem("s_done")
        chain_logits = sem("chain_logits")
        chain_sums = sem("chain_sums")
        max_ready = sem("max_ready")
        inverse_ready = sem("inverse_ready")
        shifted_ready = sem("shifted_ready")
        exp_ready = sem("exp_ready")
        probs_ready = sem("probs_ready")
        probs_turned = sem("probs_turned")
        probs_t_ready = sem("probs_t_ready")
        v_spread = sem("v_spread")
        v_masked = sem("v_masked")
        av_done = sem("av_done")
        att_t_ready = sem("att_t_ready")
        h1_done = sem("h1_done")
        h1_ready = sem("h1_ready")
        chain_residual = sem("chain_residual")
        chain_top = sem("chain_top")
        chain_gates = sem("chain_gates")
        stats_done, chain_apply, var_ready, pool_chain, rstd_ready = (
            [sem(f"{name}{k}") for k in range(3)]
            for name in ("stats_done", "chain_apply", "var_ready", "pool_chain", "rstd_ready"))
        pool_finish = sem("pool_finish")
        xn_ready = sem("xn_ready")
        xn_turned = sem("xn_turned")
        xn_split_ready = sem("xn_split_ready")
        rqk_done = sem("rqk_done")
        rv_done = sem("rv_done")
        v2_ready = sem("v2_ready")
        rot_ready = sem("rot_ready")
        qk_rotated = sem("qk_rotated")
        k_moved = sem("k_moved")
        kq_done = sem("kq_done")
        att_ready = sem("att_ready")
        k_dec_ready = sem("k_dec_ready")
        state_done = sem("state_done")
        state_ready = sem("state_ready")
        ret_done = sem("ret_done")
        h2_ready = sem("h2_ready")
        x2_ready = sem("x2_ready")
        x2_turned = sem("x2_turned")
        x2_split_ready = sem("x2_split_ready")
        gl_done = sem("gl_done")
        diff_ready = sem("diff_ready")
        gexp_ready = sem("gexp_ready")
        gates_ready = sem("gates_ready")
        gates_turned = sem("gates_turned")
        gates_split_ready = sem("gates_split_ready")
        up_done = sem("up_done")
        gate_done = sem("gate_done")
        hidden_ready = sem("hidden_ready")
        gate_copied = sem("gate_copied")
        open_done = sem("open_done")
        opened = sem("opened")
        product_ready = sem("product_ready")
        added = sem("added")
        down_done = sem("down_done")
        moe_folded = sem("moe_folded")
        moe_added = sem("moe_added")
        res_free = sem("res_free")
        chain_state = sem("chain_state")
        h3_ready = sem("h3_ready")
        stored = sem("stored")

        def due(s, odd, e, at, blocks):
            n = s - at // EXPERTS
            if at % EXPERTS == e and (not isinstance(s, int) or 0 <= n < blocks):
                yield n, (odd - at // EXPERTS) % 2

        def link(eng, s, n, per):
            count = [0]

            def wait_for(ins):
                count[0] += 1
                assert count[0] <= per
                ins.then_inc(s, 1)
                eng.wait_ge(s, n * per + count[0])
            return wait_for

        N_FILLED = 5
        SETUP_WINDOW, SETUP_RETENTION, SETUP_EXPERTS = 14, 18, 23

        def wait_parts(eng, s, split=False):
            if s == -1:
                eng.wait_ge(loaded["window"], 16)
                eng.wait_ge(loaded["retention"], 32)
                eng.wait_ge(filled, N_FILLED)
                eng.wait_ge(setup, SETUP_RETENTION)
            if s == 1:
                eng.wait_ge(loaded["rotary"], 16)
                eng.wait_ge(loaded["experts"], 16)
                if split:
                    eng.wait_ge(setup, SETUP_EXPERTS)

        block = ctx.enter_context(nc.Block())

        @block.sync
        def _(sp):
            def load_x(it):
                for half in (0, 64):
                    sp.dma_start(x_in[half:half + 64, :],
                                 I["x"][bass.ds(it, 1)].rearrange("o c t -> (o c) t")).then_inc(x_loaded, 16)

            def store(n):
                sp.wait_ge(h3_ready, n + 1)
                sp.dma_start(y[bass.ds(n * CHUNKS, CHUNKS)].rearrange("c t n -> t c n"), h3[:]).then_inc(stored, 16)

            load_x(0)
            for group in PACKED:
                sp.dma_start(packed[group][:], I[group]).then_inc(loaded[group], 16)
                if group == "retention":
                    sp.dma_start(h1[0][:].rearrange("p c n -> p (c n)"), I["cls"]).then_inc(loaded[group], 16)
            sp.wait_ge(x_ready, 1)
            load_x(1)
            sp.wait_ge(x_ready, 2)
            load_x(2)
            with sp.Fori(2, ALL_BLOCKS) as it:
                sp.wait_ge(x_ready, it + 1)
                load_x(it + 1)
                store(it - 2)
            for n in range(ALL_BLOCKS - 2, ALL_BLOCKS + 1):
                store(n)
            sp.wait_ge(stored, 16 * (ALL_BLOCKS + 2))

        @block.tensor
        def _(pe):
            mm = pe.matmul

            def w_project_qk(it):
                pe.wait_ge(x_ready, it + 1)
                if later(it):
                    pe.wait_ge(h1_ready, it)
                for out, w in ((A0[:, 0:HALF], q_even_odd), (A0[:, HALF:BT], k_even_odd)):
                    for k in range(4):
                        last = mm(out, w[k // 2][k % 2][:], x_split[:, (k // 2) * HALF:(k // 2 + 1) * HALF],
                                  start=(k == 0), stop=(k == 3))
                last.then_inc(qk_done, 1)

            def w_project_v(it):
                for t in range(4):
                    for s in range(2):
                        last = mm(A1[0:CT, t * EMB:(t + 1) * EMB], x_split[:, t * CT:(t + 1) * CT], v_w[s][:],
                                  start=(s == 0), stop=(s == 1))
                last.then_inc(v_done, 1)

            def w_scores(it):
                pe.wait_ge(q_ready, 2 * it + 2)
                pe.wait_ge(k_ready, it + 1)
                pe.wait_ge(v_masked, 4 * it + 2)
                for g in range(4):
                    for c in range(4):
                        p = 4 * g + c if 4 * g + c < PAIRS else 4 * g + c - 2
                        last = mm(A1[32 * c:32 * c + 32, g * 128:(g + 1) * 128],
                                  q_zero[:, p].rearrange("p w q -> p (w q)"),
                                  k_heads[:, p].rearrange("p h q -> p (h q)"), start=True, stop=True)
                last.then_inc(s_done, 1)

            def w_spread_v(it, j):
                if j < 2:
                    pe.wait_ge(v_ready, it + 1)
                if j == 0:
                    pe.wait_ge(k_copied, it + 1)
                    pe.wait_ge(q_ready, 2 * it + 2)
                if j == 2:
                    pe.wait_ge(v_masked, 4 * it + 1)
                if j == 3:
                    pe.wait_ge(chain_logits, it + 1)
                bank = (A0, A1)[j % 2]
                for k in range(2 * j, min(2 * j + 2, WPT)):
                    for s in range(2):
                        last = mm(bank[:, (k % 2) * 256:(k % 2) * 256 + 256], pick[:, k, :], v_parts[s][:],
                                  start=(s == 0), stop=(s == 1))
                last.then_inc(v_spread, 1)

            def w_turn_probs(it):
                pe.wait_ge(probs_ready, it + 1)
                pe.wait_ge(v_masked, 4 * it + 3)
                for g in range(4):
                    last = pe.transpose(A0[:, g * 128:(g + 1) * 128],
                                        probs_n[:, g].rearrange("p h q -> p (h q)"), ident[:])
                last.then_inc(probs_turned, 1)

            def w_values(it):
                pe.wait_ge(probs_t_ready, it + 1)
                pe.wait_ge(v_masked, 4 * it + 4)
                for p in range(PAIRS):
                    wr, k = p // WPT, p % WPT
                    for odd in range(2):
                        col = (p // 4) * 128 + (p % 4) * 32 + odd * QUERIES
                        out = A1[64 * odd:64 * odd + 64, wr * HALF:(wr + 1) * HALF].rearrange(
                            "p (a c b) -> p a c b", a=WIN, b=WIN)[:, :, 2 * k + odd, :]
                        last = mm(out, v_heads[:, k, 2 * odd + wr, :], probs_t[:, col:col + QUERIES],
                                  start=True, stop=True)
                last.then_inc(av_done, 1)

            def w_project_out(it):
                pe.wait_ge(att_t_ready, 2 * it + 2)
                for c in range(CHUNKS):
                    last = mm(A0[0:CT, c * EMB:(c + 1) * EMB], att_t[:, c * CT:(c + 1) * CT], out_w[:],
                              start=True, stop=True)
                last.then_inc(h1_done, 1)

            def r_turn(src, bank, ready, count, done):
                pe.wait_ge(ready, count)
                for c in range(CHUNKS):
                    last = pe.transpose(bank[:, c * CT:(c + 1) * CT], src[:, c].rearrange("p a n -> p (a n)").bitcast(F32),
                                        ident[0:CT, 0:CT])
                last.then_inc(done, 1)

            def r_project_qk(n):
                pe.wait_ge(xn_split_ready, n + 1)
                if later(n):
                    pe.wait_ge(gates_split_ready, n)
                for k, bank in ((0, B1), (1, B0)):
                    for s in range(2):
                        last = mm(bank[:, 0:BT], r_w[s][:, 2 * k:2 * k + 2].rearrange("p a b -> p (a b)"),
                                  xn_split[:], start=(s == 0), stop=(s == 1))
                last.then_inc(rqk_done, 1)

            def r_project_v(n):
                pe.wait_ge(rot_ready, n + 1)
                for c in range(CHUNKS):
                    for s in range(2):
                        last = mm(B1[0:CT, c * EMB:(c + 1) * EMB], xn_split[:, c * CT:(c + 1) * CT],
                                  r_w[s][:, 4], start=(s == 0), stop=(s == 1))
                last.then_inc(rv_done, 1)

            def r_scores(n):
                pe.wait_ge(rot_ready, n + 1)
                pe.wait_ge(k_moved, n + 1)
                for c in range(CHUNKS):
                    cols = slice(c * CT, (c + 1) * CT)
                    last = mm(B0[0:CT, cols], k_t[:, cols], qk_rot[0:EMB, cols], start=True, stop=True)
                last.then_inc(kq_done, 1)
                for c in range(CHUNKS):
                    pe.transpose(B1[0:CT, 256 + c * EMB:256 + (c + 1) * EMB], k_t[:, c * CT:(c + 1) * CT],
                                        ident[0:EMB, 0:EMB])

            def r_state(n):
                pe.wait_ge(v2_ready, n + 1)
                pe.wait_ge(k_dec_ready, n + 1)
                pe.wait_ge(att_ready, n + 1)
                rows = CT if later(n) else 1
                for c in range(CHUNKS):
                    last = mm(B0[0:EMB, c * EMB:(c + 1) * EMB], k_dec[0:rows, c], v2[0:rows, c],
                              start=True, stop=True)
                last.then_inc(state_done, 1)

            def r_output(n):
                for c in range(CHUNKS):
                    mm(B1[0:CT, c * EMB:(c + 1) * EMB], att[:, c], v2[:, c], start=True, stop=True)
                pe.wait_ge(state_ready, n + 1)
                for c in range(CHUNKS):
                    last = mm(B1[0:CT, 256 + c * EMB:256 + (c + 1) * EMB], qk_rot[0:EMB, c * CT:(c + 1) * CT],
                              state[:, c], start=True, stop=True)
                last.then_inc(ret_done, 1)

            def r_gate(n, buf):
                pe.wait_ge(x2_split_ready, n + 1)
                for c in range(CHUNKS):
                    for s in range(2):
                        last = mm(B1[0:CT, c * EXPERTS:(c + 1) * EXPERTS], x2_split[buf][:, c * CT:(c + 1) * CT],
                                  gate_w[s][:], start=(s == 0), stop=(s == 1))
                last.then_inc(gl_done, 1)

            def r_turn_gates(n):
                pe.wait_ge(gates_ready, n + 1)
                for c in range(CHUNKS):
                    last = pe.transpose(B0[0:2 * EXPERTS, c * CT:(c + 1) * CT],
                                        gates_parts[:, c].rearrange("p s e -> p (s e)").bitcast(F32), ident[0:CT, 0:CT])
                last.then_inc(gates_turned, 1)

            def e_open(n, buf):
                pe.wait_ge(gates_split_ready, n + 1)
                if later(n):
                    pe.wait_ge(gate_copied, COUPLES * n)
                for s in range(2):
                    last = mm(gate_ps[:, 0:BT], b2_w[s][:], gates_split[buf][:], start=(s == 0), stop=(s == 1))
                last.then_inc(open_done, 1)

            def e_up(n, e, buf):
                if e % 2 == 0 and (later(n) or e):
                    pe.wait_ge(hidden_ready, EXPERTS * n + e)
                for s in range(2):
                    last = mm(up_ps[e % 2][:, 0:BT], up_w[s][:, e], x2_split[buf][:], start=(s == 0), stop=(s == 1))
                last.then_inc(up_done, 1)

            before_fold = (PE_AT["fold"] - EXPERTS - GATE_AT) // 2 + 1
            assert 1 <= before_fold < COUPLES

            def e_spread_gate(n, j, buf):
                if j == before_fold and later(n):
                    pe.wait_ge(moe_added, n)
                elif j:
                    pe.wait_ge(gate_copied, COUPLES * n + j)
                else:
                    pe.wait_ge(opened, n + 1)
                mm(gate_ps[:, 0:BT], sel[:, 2 * j:2 * j + 2].rearrange("p e m -> p (e m)"), gates_split[buf][:],
                   start=True, stop=True).then_inc(gate_done, 1)

            def e_down(n, e):
                if e % 2 == 0:
                    pe.wait_ge(hidden_ready, EXPERTS * n + e + 2)
                    if later(n) or e:
                        pe.wait_ge(product_ready, COUPLES * n + e // 2)
                half = 64 * (e % 2)
                mm(down_ps[half:half + 64, 0:BT], down_w[:, e], hidden[:, e % HIDDEN_BUFS],
                   start=True, stop=True).then_inc(down_done, 1)

            def e_fold(n, buf):
                pe.wait_ge(added, COUPLES * (n + 1))
                last_block = isinstance(n, int) and n == ALL_BLOCKS
                pe.wait_ge(gate_copied, COUPLES * (n + 1) + (0 if last_block else before_fold))
                for c in range(CHUNKS):
                    last = mm(gate_ps[0:CT, c * EMB:(c + 1) * EMB], total[buf][:, c * CT:(c + 1) * CT], fold[:],
                              start=True, stop=True)
                last.then_inc(moe_folded, 1)

            def slot(s, odd):
                for e in range(EXPERTS):
                    def at(step, blocks=ALL_BLOCKS + 1):
                        return due(s, odd, e, step, blocks)

                    for j in range(COUPLES):
                        for n, buf in at(EXPERT_AT + 2 * j):
                            e_up(n, 2 * j, buf)
                            e_up(n, 2 * j + 1, buf)
                    for j in range(COUPLES):
                        for n, _ in at(EXPERT_AT + 2 * j + DOWN_LAG):
                            e_down(n, 2 * j)
                            e_down(n, 2 * j + 1)
                    for j in range(COUPLES):
                        for n, buf in at(GATE_AT + 2 * j): e_spread_gate(n, j, buf)
                    for it, _ in at(PE_AT["qk"], ALL_BLOCKS): w_project_qk(it)
                    for it, _ in at(PE_AT["v"], ALL_BLOCKS): w_project_v(it)
                    for j in range(2):
                        for it, _ in at(PE_AT["spread"][j], ALL_BLOCKS): w_spread_v(it, j)
                    for it, _ in at(PE_AT["scores"], ALL_BLOCKS): w_scores(it)
                    for j in range(2, 4):
                        for it, _ in at(PE_AT["spread"][j], ALL_BLOCKS): w_spread_v(it, j)
                    for it, _ in at(PE_AT["probs"], ALL_BLOCKS): w_turn_probs(it)
                    for it, _ in at(PE_AT["values"], ALL_BLOCKS): w_values(it)
                    for it, _ in at(PE_AT["out"], ALL_BLOCKS): w_project_out(it)
                    for n, _ in at(PE_AT["xn"]):
                        if later(n):
                            pe.wait_ge(diff_ready, n)
                        r_turn(xn, B1, xn_ready, n + 1, xn_turned)
                    for n, _ in at(PE_AT["rqk"]): r_project_qk(n)
                    for n, _ in at(PE_AT["rscores"]): r_scores(n)
                    for n, _ in at(PE_AT["rv"]): r_project_v(n)
                    for n, _ in at(PE_AT["state"]): r_state(n)
                    for n, _ in at(PE_AT["output"]): r_output(n)
                    for n, buf in at(PE_AT["x2"]): r_turn(x2_parts, B0, x2_ready, n + 1, x2_turned)
                    for n, buf in at(PE_AT["logits"]): r_gate(n, buf)
                    for n, _ in at(PE_AT["gates"]): r_turn_gates(n)
                    for n, buf in at(PE_AT["fold"]): e_fold(n, buf)
                    for n, buf in at(PE_AT["open"]): e_open(n, buf)

            for s in range(-1, LOOP_FROM):
                wait_parts(pe, s, True)
                slot(s, s % 2)
            with pe.Fori(LOOP_FROM // 2, ALL_BLOCKS // 2) as pair:
                slot(2 * pair, 0)
                slot(2 * pair + 1, 1)
            for s in range(ALL_BLOCKS, ALL_BLOCKS + 3):
                slot(s, s % 2)

        @block.scalar
        def _(act):
            A = act.activation

            def w_split(it):
                act.wait_ge(x_loaded, 32 * it + 32)
                if later(it):
                    act.wait_ge(v_done, it)
                A(x_split[:], x_in[:], ACT.Copy).then_inc(x_high, 1)

            def w_evac_qk(it):
                act.wait_ge(qk_done, it + 1)
                A(k_sb[:], A0[:, HALF:BT], ACT.Identity, bias=qk_bias[:, 1:2]).then_inc(k_copied, 1)
                for odd in range(2):
                    rows = slice(64 * odd, 64 * odd + 64)
                    A(q_zero[rows, :, odd, :], A0[rows, 0:HALF].rearrange("p (w q) -> p w q", q=QUERIES),
                      ACT.Identity, bias=q_bias[rows, 0:1], scale=float(HD) ** -0.5).then_inc(q_ready, 1)

            def w_evac_v(it):
                act.wait_ge(v_done, it + 1)
                A(v_parts[0][:], A1[0:CT, 0:256], ACT.Copy).then_inc(v_high, 1)

            def w_exp(it):
                act.wait_ge(shifted_ready, it + 1)
                A(probs[:], shifted[:], ACT.Exp).then_inc(exp_ready, 1)

            def w_evac_probs(it):
                act.wait_ge(probs_turned, it + 1)
                A(probs_t[:], A0[:], ACT.Copy).then_inc(probs_t_ready, 1)

            def w_evac_att(it):
                act.wait_ge(av_done, it + 1)
                for odd in range(2):
                    A(att_t[0:EMB, :].rearrange("p (a c b) -> p a c b", a=ROWS, b=WIN)[:, :, odd::2, :],
                      A1[64 * odd:64 * odd + 64, 0:BT].rearrange("p (a c b) -> p a c b", a=ROWS, b=WIN)[:, :, odd::2, :],
                      ACT.Identity, bias=v_bias[64 * odd:64 * odd + 64, 0:1]).then_inc(att_t_ready, 1)

            def w_evac_h1(it, buf):
                act.wait_ge(h1_done, it + 1)
                A(h1[buf][:].rearrange("p c n -> p (c n)"), A0[0:CT, 0:256], ACT.Copy).then_inc(h1_ready, 1)

            def r_evac_xn(n):
                act.wait_ge(xn_turned, n + 1)
                A(xn_split[:], B1[:, 0:BT], ACT.Copy).then_inc(xn_split_ready, 1)

            def r_move_k(n):
                act.wait_ge(qk_rotated, n + 1)
                A(k_t[:], qk_rot[64:128, :], ACT.Copy).then_inc(k_moved, 1)

            def r_evac_kv(n):
                variant = 0 if later(n) else 1
                act.wait_ge(rv_done, n + 1)
                A(k_dec[:].rearrange("p c n -> p (c n)"), B1[0:CT, 256:512], ACT.Copy,
                  scale=key_decay[:, variant:variant + 1]).then_inc(k_dec_ready, 1)
                A(v2[:].rearrange("p c n -> p (c n)"), B1[0:CT, 0:256], ACT.Copy).then_inc(v2_ready, 1)

            def r_evac_x2(n, buf):
                act.wait_ge(x2_turned, n + 1)
                A(x2_split[buf][:], B0[:, 0:BT], ACT.Copy).then_inc(x2_split_ready, 1)

            def r_gate_exp(n):
                act.wait_ge(diff_ready, n + 1)
                A(top_exp[:], top_diff[:], ACT.Exp).then_inc(gexp_ready, 1)

            def r_evac_gates(n, buf):
                act.wait_ge(gates_turned, n + 1)
                A(gates_split[buf][0:2 * EXPERTS, :], B0[0:2 * EXPERTS, 0:BT], ACT.Copy).then_inc(gates_split_ready, 1)

            def e_hidden(n, e):
                act.wait_ge(up_done, EXPERTS * n + e + 1)
                if later(n) or e >= HIDDEN_BUFS:
                    act.wait_ge(down_done, EXPERTS * n + e - HIDDEN_BUFS + 1)
                A(hidden[:, e % HIDDEN_BUFS], up_ps[e % 2][:, 0:BT], ACT.Relu, bias=up_bias[:, e:e + 1]).then_inc(hidden_ready, 1)

            def e_copy_gate(n, j):
                act.wait_ge(gate_done, COUPLES * n + j + 1)
                if later(n) or j >= GATE_BUFS:
                    act.wait_ge(product_ready, COUPLES * n + j - GATE_BUFS + 1)
                A(gate_rows[:, j % GATE_BUFS], gate_ps[:, 0:BT], ACT.Copy).then_inc(gate_copied, 1)

            def e_copy_open(n, buf):
                act.wait_ge(open_done, n + 1)
                A(total[buf][:], gate_ps[:, 0:BT], ACT.Copy).then_inc(opened, 1)

            def slot(s, odd):
                for e in range(EXPERTS):
                    def at(step, blocks=ALL_BLOCKS + 1):
                        return due(s, odd, e, step, blocks)

                    for it, _ in at(ACT_AT["x"]): w_split(it)
                    for k in range(EXPERTS):
                        for n, _ in at(EXPERT_AT + k): e_hidden(n, k)
                    for n, buf in at(ACT_AT["open"]): e_copy_open(n, buf)
                    for j in range(COUPLES):
                        for n, _ in at(GATE_AT + 2 * j): e_copy_gate(n, j)
                    for it, _ in at(ACT_AT["qk"], ALL_BLOCKS): w_evac_qk(it)
                    for it, _ in at(ACT_AT["v"], ALL_BLOCKS): w_evac_v(it)
                    for it, _ in at(ACT_AT["exp"], ALL_BLOCKS): w_exp(it)
                    for it, _ in at(ACT_AT["probs"], ALL_BLOCKS): w_evac_probs(it)
                    for it, _ in at(ACT_AT["values"], ALL_BLOCKS): w_evac_att(it)
                    for it, buf in at(ACT_AT["out"], ALL_BLOCKS): w_evac_h1(it, 1 - buf)
                    for n, _ in at(ACT_AT["xn"]): r_evac_xn(n)
                    for n, _ in at(ACT_AT["rotate"]): r_move_k(n)
                    for n, _ in at(ACT_AT["kv"]): r_evac_kv(n)
                    for n, buf in at(ACT_AT["x2"]): r_evac_x2(n, buf)
                    for n, _ in at(ACT_AT["exp_gate"]): r_gate_exp(n)
                    for n, buf in at(ACT_AT["gates"]): r_evac_gates(n, buf)

            for s in range(-1, LOOP_FROM):
                wait_parts(act, s)
                slot(s, s % 2)
            with act.Fori(LOOP_FROM // 2, ALL_BLOCKS // 2) as pair:
                slot(2 * pair, 0)
                slot(2 * pair + 1, 1)
            for s in range(ALL_BLOCKS, ALL_BLOCKS + 3):
                slot(s, s % 2)

        @block.vector
        def _(dve):
            TT, TS, CP = dve.tensor_tensor, dve.tensor_scalar, dve.tensor_copy

            made = [0]

            def did(ins):
                made[0] += 1
                ins.then_inc(setup, 1)

            def settle():
                dve.wait_ge(setup, made[0])

            def low(parts, raw):
                return TT(parts[1][:], raw[:], parts[0][:].bitcast(F32), ALU.subtract)

            def set_up_window():
                dve.wait_ge(loaded["window"], 16)
                dve.wait_ge(filled, N_FILLED)
                for odd in range(2):
                    cols = slice(64 * odd, 64 * odd + 64)
                    did(CP(q_even_odd[odd][0][:, cols], qk_raw[:, 0]))
                    did(CP(k_even_odd[odd][0][:, cols], qk_raw[:, 1]))
                did(CP(v_w[0][:], v_raw[:]))
                did(CP(pick[:], pick_raw[:]))
                did(TS(q_bias[:], qk_bias[:, 0:1], float(HD) ** -0.5, None, ALU.mult))
                did(dve.memset(att_t[EMB:EMB + 1, :], 1.0))
                wb = win_bias.rearrange("p a b q -> p (a b) q")
                did(TT(wb, wb, broadcast(pos_bias[:], 1, BLOCKS * 4), ALU.add))
                settle()
                for odd in range(2):
                    cols = slice(64 * odd, 64 * odd + 64)
                    did(TT(q_even_odd[odd][1][:, cols], qk_raw[:, 0], q_even_odd[odd][0][:, cols].bitcast(F32),
                           ALU.subtract))
                    did(TT(k_even_odd[odd][1][:, cols], qk_raw[:, 1], k_even_odd[odd][0][:, cols].bitcast(F32),
                           ALU.subtract))
                did(low(v_w, v_raw))
                assert made[0] == SETUP_WINDOW
                settle()

            def set_up_retention():
                dve.wait_ge(loaded["retention"], 32)
                did(CP(r_w[0][:], r_raw[:]))
                did(CP(gate_w[0][:], gate_raw[:]))
                settle()
                did(low(r_w, r_raw))
                did(low(gate_w, gate_raw))
                assert made[0] == SETUP_RETENTION
                settle()

            def set_up_experts():
                dve.wait_ge(loaded["rotary"], 16)
                dve.wait_ge(loaded["experts"], 16)
                did(CP(up_w[0][:], up_raw[:]))
                did(CP(b2_w[0][:], b2_raw[:]))
                did(CP(sel[:], broadcast(sel_row[:], 2, EMB)))
                settle()
                did(low(up_w, up_raw))
                did(low(b2_w, b2_raw))
                assert made[0] == SETUP_EXPERTS
                settle()

            def w_evac_v(it):
                dve.wait_ge(v_high, it + 1)
                TT(v_parts[1][:], A1[0:CT, 0:256], v_parts[0][:].bitcast(F32), ALU.subtract).then_inc(v_ready, 1)

            def w_softmax(it):
                ch = link(dve, chain_logits, it, 1)
                dve.wait_ge(s_done, it + 1)
                bias = win_bias[:, bass.ds(it % BLOCKS, 1)].rearrange("p o g q -> p (o g) q")
                ch(TT(logits[:], A1[:].rearrange("p (g h q) -> p g h q", g=4, h=HEADS), broadcast(bias, 2, HEADS), ALU.add))
                dve.tensor_reduce(row_max[:], logits[:], AX.X, ALU.max).then_inc(max_ready, 1)

            def w_normalise(it):
                ch = link(dve, chain_sums, it, 1)
                dve.wait_ge(exp_ready, it + 1)
                ch(dve.tensor_reduce(row_sum[:], probs[:], AX.X, ALU.add))
                dve.reciprocal(row_inv[:], row_sum[:]).then_inc(inverse_ready, 1)

            def w_mask_v(it, j):
                dve.wait_ge(v_spread, 4 * it + j + 1)
                bank = (A0, A1)[j % 2]
                m = min(2, WPT - 2 * j)
                TT(v_heads[:, 2 * j:2 * j + m].rearrange("p k t n -> p (k t) n"),
                   bank[:, 0:256 * m].rearrange("p (a n) -> p a n", n=EMB),
                   broadcast(head_columns[:], 1, 4 * m), ALU.mult).then_inc(v_masked, 1)

            def carrier():
                dve.memset(spare[:], 0.0)

            def norm_stats(src, k, n):
                for c in range(CHUNKS):
                    ins = dve.bn_stats(stats[k][:, c], src[:, c])
                ins.then_inc(stats_done[k], 1)
                dve.wait_ge(stats_done[k], n + 1)
                carrier()
                for c in range(CHUNKS):
                    ins = dve.bn_aggr(mean_var[k][:, c], stats[k][:, c])
                ins.then_inc(var_ready[k], 1)

            def norm_apply(src, k, full, parts, n, done):
                ch = link(dve, chain_apply[k], n, 2)
                dve.wait_ge(rstd_ready[k], n + 1)
                for c in range(CHUNKS):
                    ins = TS(full[:, c], src[:, c], mean_var[k][:, c, 0:1], rstd[k][:, c:c + 1], ALU.subtract, ALU.mult)
                ch(ins)
                ch(CP(parts[:, :, 0], full[:]))
                TT(parts[:, :, 1], full[:], parts[:, :, 0].bitcast(F32), ALU.subtract).then_inc(done, 1)

            def r_norm1_stats(n, buf):
                if later(n):
                    dve.wait_ge(h1_ready, n)
                norm_stats(h1[buf], 0, n)

            def r_norm1(n, buf):
                norm_apply(h1[buf], 0, xn_full, xn, n, xn_ready)

            def r_rotate(n):
                if later(n):
                    position = ((n - 1) % BLOCKS) * BT + 1
                    cos, sin = cos_t[:, bass.ds(position, BT)], sin_t[:, bass.ds(position, BT)]
                else:
                    cos, sin = cls_cos[:], cls_sin[:]
                dve.wait_ge(rqk_done, n + 1)
                TT(rot_cos[:], B1[:, 0:BT], cos, ALU.mult)
                TT(rot_sin[:], B0[:, 0:BT], sin, ALU.mult).then_inc(rot_ready, 1)

            def r_decay(n):
                variant = 0 if later(n) else 1
                dve.wait_ge(kq_done, n + 1)
                TT(att[:], B0[0:CT, 0:BT].rearrange("p (c n) -> p c n", n=CT),
                   broadcast(decay[:, variant], 1, CHUNKS), ALU.mult).then_inc(att_ready, 1)

            def r_state(n):
                if not later(n):
                    dve.wait_ge(state_done, 1)
                    CP(state_cls[:], B0[0:EMB, 0:EMB]).then_inc(state_ready, 1)
                    return
                ch = link(dve, chain_state, n - 1, 5)
                ch(TS(state_mid[:], state[:, CHUNKS], carry[:, 0, bass.ds(n, 1)], None, ALU.mult))
                ch(dve.scalar_tensor_tensor(state[:, 0], state_cls[:], carry[:, 1, bass.ds(n, 1)], state_mid[:],
                                            ALU.mult, ALU.add))
                dve.wait_ge(state_done, n + 1)
                for c in range(CHUNKS):
                    ins = dve.scalar_tensor_tensor(state[:, c + 1], state[:, c], GAMMA ** CT,
                                                   B0[0:EMB, c * EMB:(c + 1) * EMB], ALU.mult, ALU.add)
                    if c < CHUNKS - 1:
                        ch(ins)
                ins.then_inc(state_ready, 1)

            def r_residual(n, buf):
                ch = link(dve, chain_residual, n, 1)
                dve.wait_ge(ret_done, n + 1)
                ch(TT(h1_intra[:].rearrange("p c n -> p (c n)"), B1[0:CT, 0:256],
                      h1[buf][:].rearrange("p c n -> p (c n)"), ALU.add))
                if not isinstance(n, int) or n >= 2:
                    dve.wait_ge(h3_ready, n - 1)
                dve.scalar_tensor_tensor(h2[buf][:].rearrange("p c n -> p (c n)"), B1[0:CT, 256:512], query_decay[:, 0:1],
                                         h1_intra[:].rearrange("p c n -> p (c n)"), ALU.mult, ALU.add).then_inc(h2_ready, 1)

            def r_norm2_stats(n, buf):
                dve.wait_ge(h2_ready, n + 1)
                norm_stats(h2[buf], 1, n)

            def r_norm2(n, buf):
                norm_apply(h2[buf], 1, x2[buf], x2_parts, n, x2_ready)

            def r_top(n):
                ch = link(dve, chain_top, n, 5)
                dve.wait_ge(gl_done, n + 1)
                ch(TT(gate_logits[:], B1[0:CT, 0:CHUNKS * EXPERTS].rearrange("p (c e) -> p c e", e=EXPERTS),
                      broadcast(gate_bias[:], 1, CHUNKS), ALU.add))
                carrier()
                for c in range(CHUNKS):
                    ins = dve.max(top_val[:, c], gate_logits[:, c])
                ch(ins)
                TT(top_diff[:], top_val[:, :, 1], top_val[:, :, 0], ALU.subtract).then_inc(diff_ready, 1)
                for c in range(CHUNKS):
                    ins = dve.max_index(top_idx[:, c], top_val[:, c], gate_logits[:, c])
                ch(ins)
                ch(CP(top_id[:], top_idx[:, :, 0:2]))
                ch(TT(one_hot[:], broadcast(broadcast(expert_ids[:], 1, CHUNKS), 1, TOP),
                      broadcast(top_id[:].rearrange("p c k -> p k c"), 3, EXPERTS), ALU.is_equal))

            def r_gates(n):
                ch = link(dve, chain_gates, n, 6)
                dve.wait_ge(gexp_ready, n + 1)
                ch(TS(top_den[:], top_exp[:], 1.0, None, ALU.add))
                ch(dve.reciprocal(top_w[:, 0], top_den[:]))
                ch(TT(top_w[:, 1], top_w[:, 0], top_exp[:], ALU.mult))
                ch(TT(gates_a[:], one_hot[:], broadcast(top_w[:], 3, EXPERTS), ALU.mult))
                ch(TT(gates[:], gates_a[:, 0], gates_a[:, 1], ALU.add))
                ch(CP(gates_parts[:, :, 0], gates[:]))
                TT(gates_parts[:, :, 1], gates[:], gates_parts[:, :, 0].bitcast(F32), ALU.subtract).then_inc(gates_ready, 1)

            def e_product(n, j):
                dve.wait_ge(gate_copied, COUPLES * n + j + 1)
                if later(n) or j >= PRODUCT_BUFS:
                    dve.wait_ge(added, COUPLES * n + j - PRODUCT_BUFS + 1)
                dve.wait_ge(down_done, EXPERTS * n + 2 * j + 2)
                TT(products[:, j % PRODUCT_BUFS], down_ps[:, 0:BT], gate_rows[:, j % GATE_BUFS],
                   ALU.mult).then_inc(product_ready, 1)

            def e_residual(n, buf):
                dve.wait_ge(res_free, n + 1)
                dve.wait_ge(moe_folded, n + 1)
                TT(res[:].rearrange("p c n -> p (c n)"), gate_ps[0:CT, 0:256].rearrange("p (c n) -> p c n", n=EMB),
                   x2[buf][:], ALU.add).then_inc(moe_added, 1)
                dve.wait_ge(moe_added, n + 1)
                norm_stats(res, 2, n)

            def slot(s, odd):
                for e in range(EXPERTS):
                    def at(step, blocks=ALL_BLOCKS + 1):
                        return due(s, odd, e, step, blocks)

                    if isinstance(s, int) and s == 0 and e == SETUP_STEP:
                        set_up_experts()
                    for j in range(COUPLES):
                        for n, _ in at(PRODUCT_AT + 2 * j): e_product(n, j)
                    for n, buf in at(DVE_AT["added"]): e_residual(n, buf)
                    for it, _ in at(DVE_AT["v"], ALL_BLOCKS): w_evac_v(it)
                    for j in range(2):
                        for it, _ in at(DVE_AT["mask"][j], ALL_BLOCKS): w_mask_v(it, j)
                    for it, _ in at(DVE_AT["softmax"], ALL_BLOCKS): w_softmax(it)
                    for it, _ in at(DVE_AT["normalise"], ALL_BLOCKS): w_normalise(it)
                    for j in range(2, 4):
                        for it, _ in at(DVE_AT["mask"][j], ALL_BLOCKS): w_mask_v(it, j)
                    for n, _ in at(DVE_AT["rotate"]): r_rotate(n)
                    for n, _ in at(DVE_AT["decay"]): r_decay(n)
                    for n, _ in at(DVE_AT["state"]): r_state(n)
                    for n, buf in at(DVE_AT["residual"]): r_residual(n, buf)
                    for n, buf in at(DVE_AT["stats2"]): r_norm2_stats(n, buf)
                    for n, buf in at(DVE_AT["norm2"]): r_norm2(n, buf)
                    for n, _ in at(DVE_AT["top"]): r_top(n)
                    for n, _ in at(DVE_AT["gates"]): r_gates(n)
                    for n, buf in at(DVE_AT["stats1"]): r_norm1_stats(n, buf)
                    for n, buf in at(DVE_AT["norm1"]): r_norm1(n, buf)

            set_up_window()
            set_up_retention()
            for s in range(-1, LOOP_FROM):
                slot(s, s % 2)
            with dve.Fori(LOOP_FROM // 2, ALL_BLOCKS // 2) as pair:
                slot(2 * pair, 0)
                slot(2 * pair + 1, 1)
            for s in range(ALL_BLOCKS, ALL_BLOCKS + 3):
                slot(s, s % 2)

        @block.gpsimd
        def _(pool):
            TT = pool.tensor_tensor

            cleared = [q_even_odd[0][0], q_even_odd[0][1], q_even_odd[1][0], q_even_odd[1][1],
                       k_even_odd[0][0], k_even_odd[0][1], k_even_odd[1][0], k_even_odd[1][1]]
            for t in cleared:
                pool.memset(t[:].bitcast(F32), 0.0)
            for t in gates_split:
                pool.memset(t[:].bitcast(F32), 0.0)
            pool.memset(q_zero[:], 0.0).then_inc(filled, 1)
            pool.memset(state[:], 0.0).then_inc(filled, 1)
            pool.memset(cls_cos[:], 1.0).then_inc(filled, 1)
            pool.memset(cls_sin[:], 0.0).then_inc(filled, 1)
            pool.memset(eps_t[:], EPS)
            pool.memset(power[:], -0.5).then_inc(filled, 1)
            pool.memset(h3[:], 0.0).then_inc(stored, 16)
            pool.memset(res[:], 0.0).then_inc(res_free, 1)

            def w_split(it):
                pool.wait_ge(x_high, it + 1)
                TT(x_split[0:64, :], x_in[0:64, :], x_split[0:64, :].bitcast(F32), ALU.subtract).then_inc(x_ready, 1)

            def w_shift(it):
                pool.wait_ge(max_ready, it + 1)
                TT(shifted[:], logits[:], broadcast(row_max[:], 3, QUERIES), ALU.subtract).then_inc(shifted_ready, 1)

            def w_normalise(it):
                pool.wait_ge(inverse_ready, it + 1)
                TT(probs_n[:], probs[:], broadcast(row_inv[:], 3, QUERIES), ALU.mult).then_inc(probs_ready, 1)

            def r_rotate(n):
                pool.wait_ge(rot_ready, n + 1)
                TT(qk_rot[:], rot_cos[:], rot_sin[:], ALU.add).then_inc(qk_rotated, 1)

            def w_expand_k(it):
                pool.wait_ge(k_copied, it + 1)
                pool.tensor_tensor(
                    k_heads[:], broadcast(k_sb[:].rearrange("p (w q) -> p w q", q=QUERIES), 2, HEADS),
                    broadcast(broadcast(head_of_channel[:], 1, PAIRS), 3, QUERIES), ALU.mult).then_inc(k_ready, 1)

            def inverse_root(n, k):
                ch = link(pool, pool_chain[k], n, 1)
                pool.wait_ge(var_ready[k], n + 1)
                ch(TT(var_eps[k][:], mean_var[k][:, :, 1], eps_t[:], ALU.add))
                TT(rstd[k][:], var_eps[k][:], power[:], ALU.pow).then_inc(rstd_ready[k], 1)

            def e_add(n, j, buf):
                if j == 0:
                    pool.wait_ge(opened, n + 1)
                else:
                    pool.wait_ge(added, COUPLES * n + j)
                pool.wait_ge(product_ready, COUPLES * n + j + 1)
                TT(total[buf][:], total[buf][:], products[:, j % PRODUCT_BUFS], ALU.add).then_inc(added, 1)

            def e_finish(n, buf):
                ch = link(pool, pool_finish, n, 3)
                pool.wait_ge(rstd_ready[2], n + 1)
                TT(centred3[:], res[:], mean_var[2][:, :, 0:1].broadcast_to([CT, CHUNKS, EMB]), ALU.subtract).then_inc(res_free, 1)
                pool.wait_ge(res_free, n + 2)
                ch(TT(normed3[:], centred3[:], broadcast(rstd[2][:], 2, EMB), ALU.mult))
                pool.wait_ge(stored, 16 * n + 16)
                ch(TT(h3[:], normed3[:], broadcast(ln_gamma[:], 1, CHUNKS), ALU.mult))
                ch(TT(h3[:], h3[:], broadcast(ln_beta[:], 1, CHUNKS), ALU.add))
                TT(h3[:], h3[:], h2[buf][:], ALU.add).then_inc(h3_ready, 1)

            def slot(s, odd):
                for e in range(EXPERTS):
                    def at(step, blocks=ALL_BLOCKS + 1):
                        return due(s, odd, e, step, blocks)

                    for j in range(COUPLES):
                        for n, buf in at(ADD_AT + 2 * j): e_add(n, j, buf)
                    for it, _ in at(POOL_AT["x"]): w_split(it)
                    for it, _ in at(POOL_AT["shift"], ALL_BLOCKS): w_shift(it)
                    for it, _ in at(POOL_AT["normalise"], ALL_BLOCKS): w_normalise(it)
                    for n, _ in at(POOL_AT["rotate"]): r_rotate(n)
                    for n, _ in at(POOL_AT["root1"]): inverse_root(n, 0)
                    for n, _ in at(POOL_AT["root2"]): inverse_root(n, 1)
                    for n, _ in at(POOL_AT["root3"]): inverse_root(n, 2)
                    for it, _ in at(POOL_AT["keys"], ALL_BLOCKS): w_expand_k(it)
                    for n, buf in at(POOL_AT["finish"]): e_finish(n, buf)

            for s in range(-1, LOOP_FROM):
                wait_parts(pool, s)
                slot(s, s % 2)
            with pool.Fori(LOOP_FROM // 2, ALL_BLOCKS // 2) as pair:
                slot(2 * pair, 0)
                slot(2 * pair + 1, 1)
            for s in range(ALL_BLOCKS, ALL_BLOCKS + 3):
                slot(s, s % 2)


def constants():
    t = {}
    p = np.arange(128)
    f = np.float32
    rows = np.zeros((QUERIES, QUERIES))
    s = WIN * (WIN // 2)
    rows[-s:, :-s] = MASKED
    rows[:-s, -s:] = MASKED
    cols = rows.reshape(WIN, WIN, WIN, WIN).transpose(1, 0, 3, 2).reshape(QUERIES, QUERIES)
    mask = np.zeros((4, 2, QUERIES, BLOCKS, 4, QUERIES), f)
    for pair in range(PAIRS):
        g, c = divmod(pair, 4)
        wr, k = divmod(pair, WPT)
        if wr == 1:
            mask[c, :, :, BLOCKS - 1, g, :] += rows
        if k == WPT - 1:
            mask[c, 1, :, :, g, :] += cols[:, None, :]
    t["win_mask"] = mask.reshape(128, -1)
    t["head_of_channel"] = ((p[:, None] % EMB) // HD == np.arange(HEADS)).astype(f)
    t["head_columns"] = (p[:, None] // QUERIES == np.arange(EMB) // HD).astype(f)
    q = np.arange(CT)
    t["pick"] = ((q[:, None, None] // QUERIES == np.arange(WPT)[:, None]) &
                 (q[:, None, None] % QUERIES == p % QUERIES)).astype(f).reshape(CT, -1)
    t["ident"] = np.eye(128, dtype=f)
    inv = f(1.0) / np.power(f(THETA), np.arange(0, EMB, 2, dtype=f) / f(EMB), dtype=f)
    angle = np.arange(SEQ, dtype=f)[:, None] * inv[None, :]
    cos, sin = np.cos(angle).astype(f), np.sin(angle).astype(f)
    t["cos"] = np.tile(np.repeat(cos, 2, axis=1).T, (2, 1)).astype(f)
    t["sin"] = np.tile(np.stack([-sin, sin], axis=2).reshape(SEQ, EMB).T, (2, 1)).astype(f)
    n = np.arange(CT)
    diff = n[None, :] - n[:, None]
    within = np.where(diff >= 0, GAMMA ** np.maximum(diff, 0).astype(np.float64), 0.0)
    t["decay"] = np.stack([within, np.eye(CT)], axis=1).astype(f).reshape(CT, -1)
    t["key_decay"] = np.stack([GAMMA ** (CT - 1.0 - n), np.ones(CT)], axis=1).astype(f)
    t["query_decay"] = (GAMMA ** (n + 1.0))[:, None].astype(f)
    first = (np.arange(ALL_BLOCKS + 1) - 1) % BLOCKS == 0
    t["carry"] = np.tile(np.concatenate([~first, first]).astype(f), (EMB, 1))
    t["expert_ids"] = np.tile(np.arange(EXPERTS, dtype=f), (CT, 1))
    e = np.arange(EXPERTS)
    t["sel_row"] = ((p[:, None] == e) | (p[:, None] == EXPERTS + e)).astype(f)
    t["fold"] = np.tile(np.eye(EMB, dtype=f), (2, 1))
    return t


def lay_out(d):
    a = {}
    x = np.roll(d["x"], (-(WIN // 2), -(WIN // 2)), axis=(2, 3))
    x = x.reshape(IMAGES, EMB, BLOCKS, 2, WIN, WPT, 2, WIN)
    x = x.transpose(0, 2, 1, 6, 3, 5, 4, 7).reshape(ALL_BLOCKS, EMB, BT)
    a["x"] = np.concatenate([x, np.zeros_like(x[:1])], axis=0)
    w1 = d["L0_tok_w1"].reshape(HD, HEADS, 3, EMB).transpose(2, 3, 1, 0).reshape(3, EMB, EMB)
    b1 = d["L0_tok_b1"].reshape(HD, HEADS, 3).transpose(2, 1, 0).reshape(3, EMB)
    both = lambda w: np.concatenate([w, w], axis=0)
    a["w_qk"] = both(w1[0:2].transpose(1, 0, 2))
    a["w_v"] = both(w1[2])
    a["b_qk"] = both(b1[0:2].T)
    a["b_v"] = both(b1[2][:, None])
    a["w_out"] = np.concatenate([d["L0_tok_w2"].T, d["L0_tok_b2"][None]], axis=0)
    c = np.array([[i, j] for i in range(WIN) for j in range(WIN)])
    rel = c[None, :, :] - c[:, None, :] + WIN - 1
    a["pos"] = np.tile(d["L0_tok_pos_emb"][rel[..., 0], rel[..., 1]], (128 // QUERIES, 1))
    swap = np.arange(EMB) ^ 1
    wq, wk = d["L0_attn_W_Q"], d["L0_attn_W_K"]
    a["w_ret"] = both(np.stack([wq, wk, wq[:, swap], wk[:, swap], d["L0_attn_W_V"]], axis=1))
    a["w_gate"] = both(d["L0_ffn_gate_w"])
    a["b_gate"] = np.tile(d["L0_ffn_gate_b"], (CT, 1))
    a["w_up"] = both(d["L0_ffn_w1"].transpose(1, 0, 2))
    a["b_up"] = d["L0_ffn_b1"].T
    a["w_down"] = d["L0_ffn_w2"].transpose(1, 0, 2)
    a["b_down"] = np.zeros((128, 128), np.float32)
    a["b_down"][0:2 * EXPERTS, 0:EMB] = both(d["L0_ffn_b2"])
    a["gamma"] = np.tile(d["L0_ffn_gamma"], (CT, 1))
    a["beta"] = np.tile(d["L0_ffn_beta"], (CT, 1))
    a["cls"] = np.tile(d["cls_tok"].reshape(1, EMB), (CT, CHUNKS))
    tables = {**a, **constants()}
    packed = {"x": a["x"], "cls": a["cls"]}
    for group, parts in PACKED.items():
        packed[group] = np.concatenate(
            [np.pad(tables[name].reshape(rows, -1), ((0, 128 - rows), (0, 0))) for name, rows, _ in parts], axis=1)
    return {k: np.ascontiguousarray(v) for k, v in packed.items()}



def kernel(**inputs):
    import concourse.bacc as bacc
    from concourse.bass_utils import run_bass_kernel_spmd

    arrays = lay_out({k: np.asarray(v) for k, v in inputs.items()})
    nc = bacc.Bacc("TRN2", target_bir_lowering=False, num_devices=1)
    aps = {k: nc.dram_tensor("in_" + k, v.shape, mybir.dt.from_np(v.dtype), kind="ExternalInput").ap()
           for k, v in arrays.items()}
    out = nc.dram_tensor("out_y", ((ALL_BLOCKS + 1) * CHUNKS, CT, EMB), F32, kind="ExternalOutput").ap()
    build_tower(nc, aps, out)
    r = run_bass_kernel_spmd(nc, [{"in_" + k: v for k, v in arrays.items()}], core_ids=[0])
    got = np.asarray(r.results[0]["out_y"])
    cls = np.tile(got[0, 0].reshape(1, 1, EMB), (IMAGES, 1, 1))
    return np.concatenate([cls, got[CHUNKS:].reshape(IMAGES, SIDE * SIDE, EMB)], axis=1)
```
